# Optimizing a Trainium2 kernel written in Bass

```python
import numpy as np
import jax
import jax.numpy as jnp

def _softmax(x, axis=-1):
    return jax.nn.softmax(x, axis=axis)

def _gelu(x):
    return jax.nn.gelu(x, approximate=True)

def _silu(x):
    return jax.nn.silu(x)

def _sigmoid(x):
    return jax.nn.sigmoid(x)

def _layernorm(x, axis=-1, eps=1e-05):
    m = jnp.mean(x, axis=axis, keepdims=True)
    v = jnp.var(x, axis=axis, keepdims=True)
    return (x - m) / jnp.sqrt(v + eps)

def _scatter_add(tgt, idx, src, axis=0):
    return tgt.at[idx].add(src)

def _segment_sum(src, seg, n):
    return jax.ops.segment_sum(src, seg, n)
kernel_name = 'mk_sandwich_d1_jaxref_r4_1a8b54'

def setup_inputs(seed: int=0):
    np.random.seed(seed)
    _w = jnp.asarray

    def _L0_attn_setup():
        import jax, jax.numpy as jnp
        import numpy as np
        LN_EPS = 1e-05

        def _silu(x):
            return x * jax.nn.sigmoid(x)
        key = jax.random.key(seed)
        ks = jax.random.split(key, 12)
        B, L, d_model = (2, 512, 256)
        d_inner, d_state, d_conv = (512, 16, 4)
        s = lambda fan: 1.0 / np.sqrt(fan)
        A = jnp.arange(1, d_state + 1, dtype=jnp.float32)[None, :] * jnp.ones((d_inner, 1), jnp.float32)
        return {'x': jax.random.normal(ks[0], (B, L, d_model), jnp.float32), 'w_in': jax.random.normal(ks[1], (d_model, 2 * d_inner), jnp.float32) * s(d_model), 'conv_w': jax.random.normal(ks[2], (d_inner, 1, d_conv), jnp.float32) * s(d_conv), 'conv_b': jax.random.normal(ks[3], (d_inner,), jnp.float32) * 0.02, 'w_xproj': jax.random.normal(ks[4], (d_inner, 2 * d_state), jnp.float32) * s(d_inner), 'w_dt': jax.random.normal(ks[5], (d_inner, d_inner), jnp.float32) * s(d_inner), 'b_dt': jax.random.normal(ks[6], (d_inner,), jnp.float32) * 0.02, 'A_log': jnp.log(A), 'D': jnp.ones((d_inner,), jnp.float32), 'w_out': jax.random.normal(ks[7], (d_inner, d_model), jnp.float32) * s(d_inner), 'ln_g': jnp.ones((d_model,), jnp.float32), 'ln_b': jnp.zeros((d_model,), jnp.float32)}
    _L0_attn_in = _L0_attn_setup()

    def _L0_ffn_setup():
        import jax, jax.numpy as jnp
        import numpy as np
        D_MODEL = 256
        M = 64
        INNER = 16
        key = jax.random.key(seed)
        ks = jax.random.split(key, 9)

        def init(k, shape, fan_in):
            bound = 1.0 / np.sqrt(fan_in)
            return jax.random.uniform(k, shape, jnp.float32, -bound, bound)
        x = jax.random.normal(ks[0], (16, 1024, D_MODEL), dtype=jnp.float32)
        Win = init(ks[1], (D_MODEL, M), D_MODEL)
        bin_ = init(ks[2], (M,), D_MODEL)
        W1 = init(ks[3], (M, INNER), 1)
        b1 = init(ks[4], (M, INNER), 1)
        W2 = init(ks[5], (M, INNER), INNER)
        b2 = init(ks[6], (M,), INNER)
        Wout = init(ks[7], (M, D_MODEL), M)
        bout = init(ks[8], (D_MODEL,), M)
        return {'x': x, 'Win': Win, 'bin_': bin_, 'W1': W1, 'b1': b1, 'W2': W2, 'b2': b2, 'Wout': Wout, 'bout': bout}
    _L0_ffn_in = _L0_ffn_setup()
    _d = {'L0_attn_x': _L0_attn_in['x'], 'L0_attn_w_in': _L0_attn_in['w_in'], 'L0_attn_conv_w': _L0_attn_in['conv_w'], 'L0_attn_conv_b': _L0_attn_in['conv_b'], 'L0_attn_w_xproj': _L0_attn_in['w_xproj'], 'L0_attn_w_dt': _L0_attn_in['w_dt'], 'L0_attn_b_dt': _L0_attn_in['b_dt'], 'L0_attn_A_log': _L0_attn_in['A_log'], 'L0_attn_D': _L0_attn_in['D'], 'L0_attn_w_out': _L0_attn_in['w_out'], 'L0_attn_ln_g': _L0_attn_in['ln_g'], 'L0_attn_ln_b': _L0_attn_in['ln_b'], 'L0_ffn_Win': _L0_ffn_in['Win'], 'L0_ffn_bin_': _L0_ffn_in['bin_'], 'L0_ffn_W1': _L0_ffn_in['W1'], 'L0_ffn_b1': _L0_ffn_in['b1'], 'L0_ffn_W2': _L0_ffn_in['W2'], 'L0_ffn_b2': _L0_ffn_in['b2'], 'L0_ffn_Wout': _L0_ffn_in['Wout'], 'L0_ffn_bout': _L0_ffn_in['bout']}
    _x0 = _d['L0_attn_x']
    _d['L0_attn_x'] = jax.random.normal(jax.random.fold_in(jax.random.key(seed), 1), (16, 1024, 256), dtype=_x0.dtype)
    del _x0
    return _d

def reference(L0_attn_x, L0_attn_w_in, L0_attn_conv_w, L0_attn_conv_b, L0_attn_w_xproj, L0_attn_w_dt, L0_attn_b_dt, L0_attn_A_log, L0_attn_D, L0_attn_w_out, L0_attn_ln_g, L0_attn_ln_b, L0_ffn_Win, L0_ffn_bin_, L0_ffn_W1, L0_ffn_b1, L0_ffn_W2, L0_ffn_b2, L0_ffn_Wout, L0_ffn_bout):

    def _L0_attn_ref(x, w_in, conv_w, conv_b, w_xproj, w_dt, b_dt, A_log, D, w_out, ln_g, ln_b):
        import jax, jax.numpy as jnp
        import numpy as np
        LN_EPS = 1e-05

        def _silu(x):
            return x * jax.nn.sigmoid(x)
        B, L, d_model = x.shape
        d_inner = conv_w.shape[0]
        d_state = A_log.shape[1]
        d_conv = conv_w.shape[2]
        residual = x
        mu = x.mean(-1, keepdims=True)
        var = ((x - mu) ** 2).mean(-1, keepdims=True)
        xn = (x - mu) * jax.lax.rsqrt(var + LN_EPS) * ln_g + ln_b
        xz = xn @ w_in
        x_b, z = jnp.split(xz, 2, axis=-1)
        xc = jnp.transpose(x_b, (0, 2, 1))
        xc = jax.lax.conv_general_dilated(xc, conv_w, window_strides=(1,), padding=[(d_conv - 1, 0)], dimension_numbers=('NCH', 'OIH', 'NCH'), feature_group_count=d_inner)
        xc = xc + conv_b[None, :, None]
        x_b = _silu(jnp.transpose(xc, (0, 2, 1)))
        A = -jnp.exp(A_log)
        x_dbl = x_b @ w_xproj
        B_mat, C_mat = jnp.split(x_dbl, 2, axis=-1)
        dt = jax.nn.softplus(x_b @ w_dt + b_dt)

        def step(h, ins):
            dt_t, B_t, C_t, x_t = ins
            A_bar = jnp.exp(dt_t[:, :, None] * A[None])
            B_bar = dt_t[:, :, None] * B_t[:, None, :]
            h = A_bar * h + B_bar * x_t[:, :, None]
            y_t = jnp.einsum('bdn,bn->bd', h, C_t)
            return (h, y_t)
        tm = lambda a: jnp.transpose(a, (1, 0, 2))
        h0 = jnp.zeros((B, d_inner, d_state), x.dtype)
        _, y = jax.lax.scan(step, h0, (tm(dt), tm(B_mat), tm(C_mat), tm(x_b)))
        y = jnp.transpose(y, (1, 0, 2)) + D * x_b
        y = y * _silu(z)
        return y @ w_out + residual

    def _L0_ffn_ref(x, Win, bin_, W1, b1, W2, b2, Wout, bout):
        import jax, jax.numpy as jnp
        import numpy as np
        D_MODEL = 256
        M = 64
        INNER = 16
        s = jnp.einsum('btd,dm->btm', x, Win) + bin_
        h = jax.nn.relu(s[..., None] * W1 + b1)
        g = jnp.einsum('btmh,mh->btm', h, W2) + b2
        out = jnp.einsum('btm,md->btd', g, Wout) + bout
        return out
    x = L0_attn_x
    x = x + _layernorm(_L0_attn_ref(_layernorm(x, axis=-1), L0_attn_w_in, L0_attn_conv_w, L0_attn_conv_b, L0_attn_w_xproj, L0_attn_w_dt, L0_attn_b_dt, L0_attn_A_log, L0_attn_D, L0_attn_w_out, L0_attn_ln_g, L0_attn_ln_b), axis=-1)
    x = x + _layernorm(_L0_ffn_ref(_layernorm(x, axis=-1), L0_ffn_Win, L0_ffn_bin_, L0_ffn_W1, L0_ffn_b1, L0_ffn_W2, L0_ffn_b2, L0_ffn_Wout, L0_ffn_bout), axis=-1)
    return x

_drawn_inputs = setup_inputs


def setup_inputs(seed=0):
    import zlib

    import numpy as np

    out = dict(_drawn_inputs(seed))
    spreads = {'L0_attn_D': (1.0, 0.2), 'L0_attn_ln_g': (1.0, 0.2), 'L0_attn_ln_b': (0.0, 0.1)}
    factors = {'L0_attn_conv_b': 7.749, 'L0_attn_b_dt': 22.256, 'L0_ffn_bin_': 5.869}
    for name, (base, spread) in spreads.items():
        noise = np.random.default_rng([zlib.crc32(name.encode()), seed]).standard_normal(out[name].shape)
        drawn = base * np.exp(spread * noise) if base else spread * noise
        out[name] = jnp.asarray(drawn.astype(out[name].dtype))
    for name, factor in factors.items():
        out[name] = (out[name] * factor).astype(out[name].dtype)
    return out
```

```python
from contextlib import ExitStack

import concourse.bass as bass
from concourse import mybir

F32 = mybir.dt.float32
ALU = mybir.AluOpType
ACT = mybir.ActivationFunctionType

P = 128
B, L, DM = 16, 1024, 256
DI, NS, TAPS = 512, 16, 4
KM, KD = DM // P, DI // P
TT, TC = 256, 512
SUB = TT // P
TILES = B * L // TT
HALF = 8
SLOTS = HALF * KD
M, INNER = 64, 16
HH = INNER // 2
EPS = 1e-5
EXP_CAP = 2.0 ** 60
RING = 4
LAG_B, LAG_SCAN, LAG_POST, LAG_FFN = 1, 3, 5, 6


def bass_mamba_mlp_sandwich(nc, x, w_in, conv_w, conv_b, w_xproj, w_dt, b_dt, A_log, D, w_out,
                            ln_g, ln_b, Win, bin_, W1, b1, W2, b2, Wout, bout, out):
    with ExitStack() as ctx:
        def sb(name, *shape):
            return ctx.enter_context(nc.sbuf_tensor(name, list(shape), F32))

        def sem(name):
            return ctx.enter_context(nc.semaphore(name))

        b_rows = nc.dram_tensor("b_rows", [TILES, NS, TT], F32).ap()
        gates = nc.dram_tensor("gates", [TILES, P, SUB * DI], F32).ap()

        w_in_sb = sb("w_in_sb", P, KM, 2 * DI)
        w_dt_sb = sb("w_dt_sb", P, KD, DI)
        w_x_sb = sb("w_x_sb", P, KD, 2 * NS)
        w_out_sb = sb("w_out_sb", P, KD, DM)
        conv_w_sb = sb("conv_w_sb", P, KD, TAPS)
        conv_diag = sb("conv_diag", P, KD, TAPS, P)
        conv_b_sb = sb("conv_b_sb", P, KD)
        b_dt_sb = sb("b_dt_sb", P, KD)
        a_log_sb = sb("a_log_sb", P, KD, NS)
        a_exp = sb("a_exp", P, NS, KD)
        a_neg = sb("a_neg", P, NS, KD)
        d_sb = sb("d_sb", P, KD)
        g_sb = sb("g_sb", P, KM)
        beta_sb = sb("beta_sb", P, KM)
        win_sb = sb("win_sb", P, KM, 2 * M)
        bin_sb = sb("bin_sb", P, 1)
        w1_sb = sb("w1_sb", P, HH)
        b1_sb = sb("b1_sb", P, HH)
        b1f = sb("b1f", P, HH)
        w2_sb = sb("w2_sb", P, HH)
        w2_diag = sb("w2_diag", P, HH, M)
        b2_sb = sb("b2_sb", M, 1)
        wout_sb = sb("wout_sb", M + 1, DM)
        ident = sb("ident", P, P)
        ident2 = sb("ident2", P, M)
        minus_half = sb("minus_half", P, 4)

        xt = sb("xt", P, SUB, DM)
        x_stats = sb("x_stats", P, SUB, 6)
        x_mv = sb("x_mv", P, SUB, 2)
        x_norm = sb("x_norm", P, 8, 6)
        xn = sb("xn", P, SUB, DM)
        xnT = sb("xnT", P, KM, TT)
        xraw = sb("xraw", P, KD, TAPS - 1 + TT)
        tails = sb("tails", P, 5, KD, TAPS - 1)
        xb = sb("xb", P, KD, TT)
        xbD = sb("xbD", P, KD, TT)
        gate_w = sb("gate_w", P, SUB, DI)
        b_tok = sb("b_tok", P, SUB, P)
        b_rowsT = sb("b_rowsT", NS, TT)
        e_sb = sb("e_sb", P, 2, TT)

        dt_sb = sb("dt_sb", P, 2, KD, TC)
        u_sb = sb("u_sb", P, 2, KD, TC)
        c_tok = sb("c_tok", P, 3 * NS, 2 * SUB)
        acc = sb("acc", P, 4 * SUB, DI)
        b_bc = sb("b_bc", P, 2, TC)
        decay = sb("decay", P, RING, TC)
        inp = sb("inp", P, RING, TC)
        h = sb("h", P, 2, KD, TC)
        state = sb("state", P, 2, NS, KD)

        gate_r = sb("gate_r", P, SUB, DI)
        xr = sb("xr", P, SUB, DM)
        yg = sb("yg", P, SUB, DI)
        ygT = sb("ygT", P, SUB, KD, P)
        xl = sb("xl", P, SUB, DM)
        r_sb = sb("r_sb", P, SUB, DM)
        r_stats = sb("r_stats", P, SUB, 6)
        r_mv = sb("r_mv", P, SUB, 2)
        r_std = sb("r_std", P, 2, SUB)
        rn = sb("rn", P, SUB, DM)
        x1 = sb("x1", P, 2, SUB, DM)
        x1_stats = sb("x1_stats", P, SUB, 6)
        x1_mv = sb("x1_mv", P, SUB, 2)
        x1_std = sb("x1_std", P, 2, SUB)
        x1n = sb("x1n", P, SUB, DM)
        x1nT = sb("x1nT", P, KM, TT)
        hid = sb("hid", P, 2, TT)
        gT = sb("gT", M + 1, TT)
        f_stats = sb("f_stats", P, SUB, 6)
        f_mv = sb("f_mv", P, SUB, 2)
        f_std = sb("f_std", P, 2, SUB)
        f_shift = sb("f_shift", P, SUB)
        fo = sb("fo", P, SUB, DM)
        x2 = sb("x2", P, SUB, DM)

        def bank(name):
            return ctx.enter_context(nc.psum_tensor(name, [P, 512], F32))

        hT_bank = [bank("hT0"), bank("hT1")]
        lo_bank, hi_bank = bank("lo_bank"), bank("hi_bank")
        mix0, mix1 = bank("mix0"), bank("mix1")
        post_bank, ffn_bank = bank("post_bank"), bank("ffn_bank")

        weights_in = sem("weights_in")
        waits_taken = sem("waits_taken")
        const_pool = sem("const_pool")
        const_act = sem("const_act")
        const_dve = sem("const_dve")
        x_in = sem("x_in")
        x_step = sem("x_step")
        x_rstd = sem("x_rstd")
        xn_ready = sem("xn_ready")
        xT_done = sem("xT_done")
        xnT_ready = sem("xnT_ready")
        xh_done = sem("xh_done")
        xraw_ready = sem("xraw_ready")
        head_ready = sem("head_ready")
        tail_saved = sem("tail_saved")
        conv_done = sem("conv_done")
        z_done = sem("z_done")
        xb_ready = sem("xb_ready")
        gate_ready = sem("gate_ready")
        gate_stored = sem("gate_stored")
        bc_done = sem("bc_done")
        c_ready = sem("c_ready")
        bT_done = sem("bT_done")
        bT_ready = sem("bT_ready")
        b_stored = sem("b_stored")
        dt_mm = sem("dt_mm")
        e_ready = sem("e_ready")
        e_capped = sem("e_capped")
        l_ready = sem("l_ready")
        dt_ready = sem("dt_ready")
        u_ready = sem("u_ready")
        xbD_ready = sem("xbD_ready")
        xbDT_done = sem("xbDT_done")
        acc_init = sem("acc_init")
        b_bc_in = [sem("b_bc_in0"), sem("b_bc_in1")]
        decay_ready = sem("decay_ready")
        inp_ready = sem("inp_ready")
        scan_done = sem("scan_done")
        state_saved = sem("state_saved")
        hT_done = sem("hT_done")
        acc_done = sem("acc_done")
        gate_in = sem("gate_in")
        xr_in = sem("xr_in")
        yg_ready = sem("yg_ready")
        ygT_done = sem("ygT_done")
        ygT_ready = sem("ygT_ready")
        proj_done = sem("proj_done")
        r_step = sem("r_step")
        r_rstd = sem("r_rstd")
        rn_ready = sem("rn_ready")
        x1_ready = sem("x1_ready")
        x1_step = sem("x1_step")
        x1_rstd = sem("x1_rstd")
        x1n_ready = sem("x1n_ready")
        x1T_done = sem("x1T_done")
        x1nT_ready = sem("x1nT_ready")
        s_done = sem("s_done")
        hid_ready = sem("hid_ready")
        hid_used = sem("hid_used")
        gT_ready = sem("gT_ready")
        f_done = sem("f_done")
        f_step = sem("f_step")
        f_rstd = sem("f_rstd")
        f_shifted = sem("f_shifted")
        fo_ready = sem("fo_ready")
        x2_ready = sem("x2_ready")
        out_stored = sem("out_stored")

        def wait(eng, s, value):
            if not isinstance(value, int) or value > 0:
                eng.wait_ge(s, value)

        def take_waits(pool):
            pool.sem_inc(waits_taken, 1)

        x_tiles = x.rearrange("b (t s p) m -> (b t) p s m", p=P, s=SUB)
        out_tiles = out.rearrange("b (t s p) m -> (b t) p s m", p=P, s=SUB)

        n_it = TILES + LAG_FFN
        edges = sorted({0, LAG_B, LAG_B + 1, LAG_SCAN, LAG_SCAN + 1, LAG_POST, LAG_FFN, LAG_FFN + 1, TILES, TILES + LAG_B,
                        TILES + LAG_SCAN, TILES + LAG_SCAN + 1, TILES + LAG_POST, n_it})

        def over_iterations(eng, body):
            for lo, hi in zip(edges, edges[1:]):
                stages = {
                    "prep_a": lo < TILES,
                    "prep_b": LAG_B <= lo < TILES + LAG_B,
                    "scan": LAG_SCAN <= lo < TILES + LAG_SCAN,
                    "before": LAG_SCAN < lo < TILES + LAG_SCAN,
                    "drain": lo == TILES + LAG_SCAN,
                    "post": LAG_POST <= lo < TILES + LAG_POST,
                    "ffn": LAG_FFN <= lo,
                }
                if hi - lo == 1:
                    body(lo, stages)
                else:
                    with eng.Fori(lo, hi) as it:
                        body(it, stages)

        def adds(s, stages, i, before):
            return (stages["scan"] and (i > 0 or stages["before"])) or (stages["drain"] and i == 0)

        block = ctx.enter_context(nc.Block())

        @block.sync
        def _(sp):
            n_w = 0
            for dst, src in (
                (w_in_sb[:, :, :], w_in.rearrange("(k p) n -> p k n", p=P)),
                (w_dt_sb[:, :, :], w_dt.rearrange("(k p) n -> p k n", p=P)),
                (w_x_sb[:, :, :], w_xproj.rearrange("(k p) n -> p k n", p=P)),
                (w_out_sb[:, :, :], w_out.rearrange("(k p) n -> p k n", p=P)),
                (conv_w_sb[:, :, :], conv_w.rearrange("(k p) o c -> p k (o c)", p=P)),
                (conv_b_sb[:, :], conv_b.rearrange("(k p) -> p k", p=P)),
                (b_dt_sb[:, :], b_dt.rearrange("(k p) -> p k", p=P)),
                (a_log_sb[:, :, :], A_log.rearrange("(k p) n -> p k n", p=P)),
                (d_sb[:, :], D.rearrange("(k p) -> p k", p=P)),
                (g_sb[:, :], ln_g.rearrange("(k p) -> p k", p=P)),
                (beta_sb[:, :], ln_b.rearrange("(k p) -> p k", p=P)),
                (win_sb[:, :, 0:M], Win.rearrange("(k p) n -> p k n", p=P)),
                (win_sb[:, :, M:2 * M], Win.rearrange("(k p) n -> p k n", p=P)),
                (bin_sb[0:M, :], bin_.rearrange("(m o) -> m o", o=1)),
                (bin_sb[M:2 * M, :], bin_.rearrange("(m o) -> m o", o=1)),
                (w1_sb[0:M, :], W1[:, 0:HH]), (w1_sb[M:2 * M, :], W1[:, HH:INNER]),
                (b1_sb[0:M, :], b1[:, 0:HH]), (b1_sb[M:2 * M, :], b1[:, HH:INNER]),
                (w2_sb[0:M, :], W2[:, 0:HH]), (w2_sb[M:2 * M, :], W2[:, HH:INNER]),
                (b2_sb[:, :], b2.rearrange("(m o) -> m o", o=1)),
                (wout_sb[0:M, :], Wout),
                (wout_sb[M:M + 1, :], bout.rearrange("(o n) -> o n", o=1)),
            ):
                sp.dma_start(dst, src, allow_slow_non_contiguous=True).then_inc(weights_in, 16)
                n_w += 1
            assert n_w == N_WEIGHTS

            def body(it, st):
                tile_a, tile_b, half, tile_p, tile_f = it, it - 1, it - LAG_SCAN, it - LAG_POST, it - LAG_FFN
                for s in range(SLOTS):
                    i = s // KD
                    if st["prep_a"] and s == 0:
                        wait(sp, xn_ready, tile_a)
                        sp.dma_start(xt[:, :, :], x_tiles[tile_a]).then_inc(x_in, 16)
                    if st["scan"] and s % KD == 0:
                        n, chunk = (half * HALF + i) % NS, half // 2
                        wait(sp, inp_ready, half * SLOTS + (i - 1) * KD)
                        if i == 0:
                            wait(sp, b_stored, chunk * 32 + 32)
                        rows = b_rows.rearrange("(c t) n k -> c n t k", t=2)[chunk, n]
                        sp.dma_start(b_bc[:, i % 2, :].rearrange("p (t k) -> p t k", t=2),
                                     rows.unsqueeze(0).broadcast_to([P, 2, TT])).then_inc(b_bc_in[i % 2], 16)
                    if st["post"] and s == 1:
                        wait(sp, gate_stored, tile_p * 16 + 16)
                        wait(sp, yg_ready, tile_p)
                        sp.dma_start(gate_r[:, :, :].rearrange("p s d -> p (s d)"), gates[tile_p]).then_inc(gate_in, 16)
                        wait(sp, x1_ready, tile_p)
                        sp.dma_start(xr[:, :, :], x_tiles[tile_p]).then_inc(xr_in, 16)
                    if st["ffn"] and s == 21:
                        wait(sp, x2_ready, tile_f + 1)
                        sp.dma_start(out_tiles[tile_f], x2[:, :, :]).then_inc(out_stored, 16)
                    if st["prep_a"] and s == 29:
                        wait(sp, gate_ready, tile_a + 1)
                        sp.dma_start(gates[tile_a], gate_w[:, :, :].rearrange("p s d -> p (s d)")).then_inc(gate_stored, 16)
                    if st["prep_a"] and s == 31:
                        wait(sp, bT_ready, tile_a + 1)
                        sp.dma_start(b_rows[tile_a], b_rowsT[:, :]).then_inc(b_stored, 16)

            over_iterations(sp, body)
            sp.wait_ge(out_stored, TILES * 16)
            sp.wait_ge(gate_stored, TILES * 16)
            sp.wait_ge(b_stored, TILES * 16)

        @block.gpsimd
        def _(pool):
            pool.memset(ident[:, :], 0.0)
            pool.memset(ident2[:, :], 0.0)
            pool.memset(minus_half[:, :], -0.5)
            pool.memset(tails[:, 0, :, :], 0.0)
            pool.memset(state[:, 0, :, :], 0.0)
            pool.memset(b_tok[:, :, :], 0.0).then_inc(const_pool, 1)
            pool.wait_ge(const_pool, 1)
            pool.affine_select(out=ident[:, :], in_=ident[:, :], compare_op=ALU.not_equal, fill=1.0,
                               base=0, pattern=[[-1, P]], channel_multiplier=1)
            pool.affine_select(out=ident2[:, :], in_=ident2[:, :], compare_op=ALU.not_equal, fill=1.0,
                               base=0, pattern=[[-1, M]], channel_multiplier=1).then_inc(const_pool, 1)
            pool.wait_ge(const_pool, 2)
            pool.affine_select(out=ident2[:, :], in_=ident2[:, :], compare_op=ALU.not_equal, fill=1.0,
                               base=-M, pattern=[[-1, M]], channel_multiplier=1).then_inc(const_pool, 1)

            def body(it, st):
                tile_a, tile_b, half, tile_p, tile_f = it, it - 1, it - LAG_SCAN, it - LAG_POST, it - LAG_FFN
                for s in range(SLOTS):
                    i, d = s // KD, s % KD
                    if st["prep_a"] and s == 4:
                        pool.wait_ge(x_step, tile_a + 1)
                        v = x_norm[:, tile_a % 8, 2:6]
                        take_waits(pool)
                        pool.tensor_tensor(v, v, minus_half[:, :], ALU.pow).then_inc(x_rstd, 1)
                    if st["prep_a"] and s == 12:
                        wait(pool, conv_done, tile_a)
                        wait(pool, tail_saved, tile_a)
                        take_waits(pool)
                        pool.tensor_copy(xraw[:, :, 0:TAPS - 1], tails[:, tile_a % 4, :, :]).then_inc(head_ready, 1)
                    if st["prep_a"] and s == 16:
                        pool.wait_ge(xraw_ready, 2 * tile_a + 2)
                        pool.wait_ge(head_ready, tile_a + 1)
                        take_waits(pool)
                        pool.tensor_copy(tails[:, tile_a % 4 + 1, :, :], xraw[:, :, TT:TT + TAPS - 1]).then_inc(tail_saved, 1)
                    if st["prep_b"] and s in (7, 11):
                        q = (s == 11)
                        pool.wait_ge(dt_ready, 2 * tile_b + 1 + q)
                        pool.wait_ge(xb_ready, tile_b + 1)
                        if q == 0:
                            if st["scan"]:
                                wait(pool, inp_ready, (tile_b - 2) // 2 * (2 * SLOTS))
                        cols = slice(tile_b % 2 * TT, tile_b % 2 * TT + TT)
                        t0 = (tile_b % 2) * TT
                        take_waits(pool)
                        pool.tensor_tensor(u_sb[:, tile_b // 2 % 2, 2 * q:2 * q + 2, bass.ds(t0, TT)],
                                           dt_sb[:, tile_b // 2 % 2, 2 * q:2 * q + 2, bass.ds(t0, TT)],
                                           xb[:, 2 * q:2 * q + 2, :], ALU.mult).then_inc(u_ready, 1)
                    if st["post"] and s == 5:
                        pool.wait_ge(gate_in, 16 * tile_p + 16)
                        pool.wait_ge(acc_done, ((tile_p // 2) * NS + NS - 1) * 4 + (tile_p % 2) * SUB + SUB)
                        wait(pool, ygT_done, 2 * tile_p)
                        take_waits(pool)
                        pool.tensor_tensor(yg[:, :, :], acc[:, bass.ds((tile_p % 4) * SUB, SUB), :],
                                           gate_r[:, :, :], ALU.mult).then_inc(yg_ready, 1)
                    if st["post"] and s == 25:
                        pool.wait_ge(r_step, 3 * tile_p + 3)
                        pool.tensor_tensor(r_std[:, 1, :], r_std[:, 0, :], minus_half[:, 0:SUB], ALU.pow).then_inc(r_rstd, 1)
                    if st["post"] and s == 27:
                        pool.wait_ge(rn_ready, tile_p + 1)
                        pool.wait_ge(xr_in, 16 * tile_p + 16)
                        wait(pool, x2_ready, tile_p - 1)
                        take_waits(pool)
                        pool.tensor_tensor(x1[:, tile_p % 2, :, :], xr[:, :, :], rn[:, :, :], ALU.add).then_inc(x1_ready, 1)
                    if st["post"] and s == 29:
                        pool.wait_ge(x1_step, tile_p + 1)
                        pool.tensor_tensor(x1_std[:, 1, :], x1_std[:, 0, :], minus_half[:, 0:SUB], ALU.pow).then_inc(x1_rstd, 1)
                    if st["ffn"] and s == 16:
                        pool.wait_ge(f_step, tile_f + 1)
                        pool.tensor_tensor(f_std[:, 1, :], f_std[:, 0, :], minus_half[:, 0:SUB], ALU.pow).then_inc(f_rstd, 1)
                    if st["ffn"] and s == 19:
                        pool.wait_ge(fo_ready, tile_f + 1)
                        wait(pool, out_stored, 16 * tile_f)
                        take_waits(pool)
                        pool.tensor_tensor(x2[:, :, :], x1[:, tile_f % 2, :, :], fo[:, :, :], ALU.add).then_inc(x2_ready, 1)
                    if st["scan"]:
                        chunk = half // 2
                        if d == 0:
                            pool.wait_ge(b_bc_in[i % 2], (half * (HALF // 2) + i // 2) * 16 + 16)
                        if s == 0:
                            pool.wait_ge(u_ready, chunk * 4 + 4)
                        wait(pool, scan_done, half * SLOTS + s - RING + 1)
                        take_waits(pool)
                        pool.tensor_tensor(inp[:, s % RING, :], u_sb[:, chunk % 2, d, :], b_bc[:, i % 2, :],
                                           ALU.mult).then_inc(inp_ready, 1)

            over_iterations(pool, body)

        @block.scalar
        def _(act):
            act.wait_ge(weights_in, 16 * N_WEIGHTS)
            act.activation(a_exp[:, :, :].rearrange("p n k -> p k n"), a_log_sb[:, :, :], ACT.Exp).then_inc(const_act, 1)
            act.wait_ge(const_dve, 1)

            def body(it, st):
                tile_a, tile_b, half, tile_p, tile_f = it, it - 1, it - LAG_SCAN, it - LAG_POST, it - LAG_FFN
                for s in range(SLOTS):
                    i, d = s // KD, s % KD
                    if st["scan"]:
                        chunk = half // 2
                        if s == 0:
                            act.wait_ge(dt_ready, chunk * 4 + 4)
                        wait(act, scan_done, half * SLOTS + s - RING + 1)
                        act.activation(decay[:, s % RING, :], dt_sb[:, chunk % 2, d, :], ACT.Exp,
                                       scale=a_neg[:, (half * HALF + i) % NS, d:d + 1]).then_inc(decay_ready, 1)
                    if st["prep_b"] and s in (4, 8):
                        q = (s == 8)
                        act.wait_ge(dt_mm, 2 * tile_b + 1 + q)
                        wait(act, dt_ready, 2 * tile_b + q)
                        bnk = (lo_bank, hi_bank)[q]
                        for k in range(2):
                            a = act.activation(e_sb[:, k, :], bnk[:, k * TT:(k + 1) * TT], ACT.Exp,
                                               bias=b_dt_sb[:, 2 * q + k:2 * q + k + 1])
                        a.then_inc(e_ready, 1)
                    if st["prep_b"] and s in (5, 9):
                        q = (s == 9)
                        act.wait_ge(e_capped, 2 * tile_b + 1 + q)
                        act.activation(e_sb[:, :, :], e_sb[:, :, :], ACT.Ln, bias=1.0).then_inc(l_ready, 1)
                    if st["prep_b"] and s == 6:
                        act.wait_ge(xb_ready, tile_b + 1)
                        wait(act, xbDT_done, 2 * tile_b)
                        for k in range(KD):
                            a = act.activation(xbD[:, k, :], xb[:, k, :], ACT.Copy, scale=d_sb[:, k:k + 1])
                        a.then_inc(xbD_ready, 1)
                    if st["prep_b"] and s in (9, 10):
                        q = (s == 10)
                        act.wait_ge(xbDT_done, 2 * tile_b + 1 + q)
                        if st["scan"]:
                            wait(act, yg_ready, tile_b - 3)
                        act.activation(acc[:, bass.ds((tile_b % 4) * SUB + q, 1), :].rearrange("p o d -> p (o d)"),
                                       (mix0, mix1)[q][:, :], ACT.Copy).then_inc(acc_init, 1)
                    if st["prep_a"] and s == 11:
                        act.wait_ge(xT_done, tile_a + 1)
                        wait(act, z_done, tile_a)
                        for k in range(KM):
                            a = act.activation(xnT[:, k, :], mix0[:, k * TT:(k + 1) * TT], ACT.Identity,
                                               scale=g_sb[:, k:k + 1], bias=beta_sb[:, k:k + 1])
                        a.then_inc(xnT_ready, 1)
                    if st["prep_a"] and s in (13, 15):
                        q = (s == 15)
                        act.wait_ge(xh_done, 2 * tile_a + 1 + q)
                        wait(act, conv_done, tile_a)
                        wait(act, tail_saved, tile_a)
                        act.activation(xraw[:, 2 * q:2 * q + 2, TAPS - 1:],
                                       (mix1, mix0)[q][:, :].rearrange("p (k t) -> p k t", k=2), ACT.Copy)\
                           .then_inc(xraw_ready, 1)
                    if st["prep_a"] and s == 27:
                        act.wait_ge(conv_done, tile_a + 1)
                        wait(act, u_ready, 2 * tile_a)
                        wait(act, xbD_ready, tile_a)
                        wait(act, dt_mm, 2 * tile_a)
                        for k in range(KD):
                            a = act.activation(xb[:, k, :], (lo_bank, hi_bank)[k // 2][:, k % 2 * TT:k % 2 * TT + TT],
                                               ACT.Silu, bias=conv_b_sb[:, k:k + 1])
                        a.then_inc(xb_ready, 1)
                        act.wait_ge(z_done, tile_a + 1)
                        wait(act, gate_stored, 16 * tile_a)
                        for q in range(SUB):
                            a = act.activation(gate_w[:, q, :], (mix1, mix0)[q][:, :], ACT.Silu)
                        a.then_inc(gate_ready, 1)
                    if st["prep_a"] and s == 30:
                        act.wait_ge(bc_done, tile_a + 1)
                        if st["scan"]:
                            wait(act, acc_done, (tile_a - 4) // 2 * (NS * 4))
                        wait(act, bT_done, tile_a)
                        bc = mix0[:, 0:SUB * 2 * NS].rearrange("p (s n) -> p s n", s=SUB)
                        act.activation(b_tok[:, :, 0:NS], bc[:, :, 0:NS], ACT.Copy)
                        act.activation(c_tok[:, bass.ds((tile_a // 2 % 3) * NS, NS), bass.ds((tile_a % 2) * SUB, SUB)]
                                       .rearrange("p n s -> p s n"), bc[:, :, NS:2 * NS], ACT.Copy).then_inc(c_ready, 1)
                    if st["prep_a"] and s == 31:
                        act.wait_ge(bT_done, tile_a + 1)
                        wait(act, b_stored, 16 * tile_a)
                        act.activation(b_rowsT[:, :], mix0[0:NS, 0:TT], ACT.Copy).then_inc(bT_ready, 1)
                    if st["post"] and s in (12, 14):
                        q = (s == 14)
                        act.wait_ge(ygT_done, 2 * tile_p + 1 + q)
                        wait(act, proj_done, tile_p)
                        act.activation(ygT[:, q, :, :], post_bank[:, :].rearrange("p (k t) -> p k t", k=KD),
                                       ACT.Copy).then_inc(ygT_ready, 1)
                    if st["ffn"] and s == 0:
                        act.wait_ge(x1T_done, tile_f + 1)
                        wait(act, s_done, tile_f)
                        act.activation(x1nT[:, :, :], post_bank[:, :].rearrange("p (k t) -> p k t", k=KM),
                                       ACT.Copy).then_inc(x1nT_ready, 1)
                    if st["ffn"] and 3 <= s < 3 + HH:
                        k = s - 3
                        if k == 0:
                            act.wait_ge(s_done, tile_f + 1)
                        wait(act, hid_used, HH * tile_f + max(k - 1, 0))
                        act.activation(hid[:, k % 2, :], post_bank[:, 0:TT], ACT.Relu, scale=w1_sb[:, k:k + 1],
                                       bias=b1f[:, k:k + 1]).then_inc(hid_ready, 1)
                    if st["ffn"] and s == 12:
                        act.wait_ge(hid_used, HH * tile_f + HH)
                        wait(act, f_done, tile_f)
                        act.activation(gT[0:M, :], ffn_bank[0:M, 0:TT], ACT.Identity, bias=b2_sb[:, :]).then_inc(gT_ready, 1)
                    if st["ffn"] and s == 18:
                        act.wait_ge(f_shifted, tile_f + 1)
                        wait(act, x2_ready, tile_f)
                        for q in range(SUB):
                            a = act.activation(fo[:, q, :], ffn_bank[:, q * DM:(q + 1) * DM], ACT.Identity,
                                               scale=f_std[:, 1, q:q + 1], bias=f_shift[:, q:q + 1])
                        a.then_inc(fo_ready, 1)

            over_iterations(act, body)

        @block.tensor
        def _(pe):
            pe.wait_ge(weights_in, 16 * N_WEIGHTS)
            pe.wait_ge(const_pool, 3)
            pe.wait_ge(const_dve, 2)

            def transpose_to(out_ap, in_ap):
                return pe.transpose(out_ap, in_ap, ident[:, :])

            def body(it, st):
                tile_a, tile_b, half, tile_p, tile_f = it, it - 1, it - LAG_SCAN, it - LAG_POST, it - LAG_FFN
                for s in range(SLOTS):
                    i, d = s // KD, s % KD
                    if adds(s, st, i, None):
                        step = half * HALF + i - 1
                        idx = step * 4 + d
                        if d == 0:
                            pe.wait_ge(scan_done, (step + 1) * KD)
                        wait(pe, acc_done, idx - 1)
                        bnk = hT_bank[d % 2]
                        hb = (i - 1) % 2
                        for k in range(KD):
                            t = transpose_to(bnk[:, k * P:(k + 1) * P], h[:, hb, k, d * P:(d + 1) * P])
                        t.then_inc(hT_done, 1)
                    if st["prep_b"] and s < 2 * KD:
                        k, kk = s // 2, s % 2
                        bnk = (lo_bank, hi_bank)[k // 2]
                        if s == 0:
                            pe.wait_ge(xb_ready, tile_b + 1)
                        for c in (2 * kk, 2 * kk + 1):
                            m = pe.matmul(bnk[:, k % 2 * TT:k % 2 * TT + TT], w_dt_sb[:, c, k * P:(k + 1) * P], xb[:, c, :],
                                          start=(c == 0), stop=(c == KD - 1))
                        if k % 2 and kk:
                            m.then_inc(dt_mm, 1)
                    if st["prep_b"] and s in (8, 9):
                        q = s - 8
                        if q == 0:
                            pe.wait_ge(xbD_ready, tile_b + 1)
                            pe.wait_ge(bT_ready, tile_b + 1)
                            pe.wait_ge(gate_ready, tile_b + 1)
                        for k in range(KD):
                            t = transpose_to((mix0, mix1)[q][:, k * P:(k + 1) * P], xbD[:, k, q * P:(q + 1) * P])
                        t.then_inc(xbDT_done, 1)
                    if st["prep_a"] and s == 10:
                        pe.wait_ge(xn_ready, tile_a + 1)
                        wait(pe, acc_init, 2 * (tile_a - 1) + 1)
                        for k in range(KM):
                            for q in range(SUB):
                                t = transpose_to(mix0[:, k * TT + q * P:k * TT + (q + 1) * P], xn[:, q, k * P:(k + 1) * P])
                        t.then_inc(xT_done, 1)
                    if st["prep_a"] and 11 <= s < 15:
                        k = s - 11
                        if k == 0:
                            pe.wait_ge(xnT_ready, tile_a + 1)
                            wait(pe, acc_init, 2 * tile_a)
                        bnk = (mix1, mix0)[k // 2]
                        for c in range(KM):
                            m = pe.matmul(bnk[:, k % 2 * TT:k % 2 * TT + TT], w_in_sb[:, c, k * P:(k + 1) * P], xnT[:, c, :],
                                          start=(c == 0), stop=(c == KM - 1))
                        if k % 2:
                            m.then_inc(xh_done, 1)
                    if st["prep_a"] and 15 <= s < 23:
                        k, kk = (s - 15) // 2, (s - 15) % 2
                        if s == 15:
                            pe.wait_ge(head_ready, tile_a + 1)
                            wait(pe, dt_ready, 2 * tile_a)
                        if k % 2 == 0 and kk == 0:
                            pe.wait_ge(xraw_ready, 2 * tile_a + 1 + k // 2)
                        bnk = (lo_bank, hi_bank)[k // 2]
                        for c in (2 * kk, 2 * kk + 1):
                            m = pe.matmul(bnk[:, k % 2 * TT:k % 2 * TT + TT], conv_diag[:, k, c, :], xraw[:, k, c:c + TT],
                                          start=(c == 0), stop=(c == TAPS - 1))
                        if s == 22:
                            m.then_inc(conv_done, 1)
                    if st["prep_a"] and 23 <= s < 27:
                        q, c = (s - 23) // 2, (s - 23) % 2
                        if s == 23:
                            pe.wait_ge(xraw_ready, 2 * tile_a + 2)
                        m = pe.matmul((mix1, mix0)[q][:, :], xnT[:, c, q * P:(q + 1) * P], w_in_sb[:, c, DI:2 * DI],
                                      start=(c == 0), stop=(c == KM - 1))
                        if s == 26:
                            m.then_inc(z_done, 1)
                    if st["prep_a"] and s == 29:
                        pe.wait_ge(xb_ready, tile_a + 1)
                        pe.wait_ge(gate_ready, tile_a + 1)
                        for q in range(SUB):
                            for c in range(KD):
                                m = pe.matmul(mix0[:, q * 2 * NS:(q + 1) * 2 * NS], xb[:, c, q * P:(q + 1) * P], w_x_sb[:, c, :],
                                              start=(c == 0), stop=(c == KD - 1))
                        m.then_inc(bc_done, 1)
                    if st["prep_a"] and s == 30:
                        pe.wait_ge(c_ready, tile_a + 1)
                        for q in range(SUB):
                            t = transpose_to(mix0[:, q * P:(q + 1) * P], b_tok[:, q, :])
                        t.then_inc(bT_done, 1)
                    if st["post"] and s in (11, 13):
                        q = (s == 13)
                        if q == 0:
                            pe.wait_ge(yg_ready, tile_p + 1)
                            wait(pe, hid_ready, HH * (tile_p - 1) + HH)
                        else:
                            pe.wait_ge(ygT_ready, 2 * tile_p + 1)
                        for k in range(KD):
                            t = transpose_to(post_bank[:, k * P:(k + 1) * P], yg[:, q, k * P:(k + 1) * P])
                        t.then_inc(ygT_done, 1)
                    if st["post"] and 15 <= s < 23:
                        q, c = (s - 15) // KD, (s - 15) % KD
                        if s == 15:
                            pe.wait_ge(ygT_ready, 2 * tile_p + 2)
                        m = pe.matmul(post_bank[:, q * DM:(q + 1) * DM], ygT[:, q, c, :], w_out_sb[:, c, :],
                                      start=(c == 0), stop=(c == KD - 1))
                        if s == 22:
                            m.then_inc(proj_done, 1)
                    if st["post"] and s == 31:
                        pe.wait_ge(x1n_ready, tile_p + 1)
                        pe.wait_ge(r_step, 3 * tile_p + 2)
                        for k in range(KM):
                            for q in range(SUB):
                                t = transpose_to(post_bank[:, k * TT + q * P:k * TT + (q + 1) * P], x1n[:, q, k * P:(k + 1) * P])
                        t.then_inc(x1T_done, 1)
                    if st["ffn"] and s == 2:
                        pe.wait_ge(x1nT_ready, tile_f + 1)
                        for c in range(KM):
                            m = pe.matmul(post_bank[:, 0:TT], win_sb[:, c, :], x1nT[:, c, :], start=(c == 0), stop=(c == KM - 1))
                        m.then_inc(s_done, 1)
                    if st["ffn"] and 4 <= s < 4 + HH:
                        k = s - 4
                        pe.wait_ge(hid_ready, HH * tile_f + k + 1)
                        if k == 0:
                            wait(pe, fo_ready, tile_f)
                        pe.matmul(ffn_bank[0:M, 0:TT], w2_diag[:, k, :], hid[:, k % 2, :], start=(k == 0),
                                  stop=(k == HH - 1)).then_inc(hid_used, 1)
                    if st["ffn"] and s in (13, 14):
                        q = s - 13
                        if q == 0:
                            pe.wait_ge(gT_ready, tile_f + 1)
                        m = pe.matmul(ffn_bank[:, q * DM:(q + 1) * DM], gT[:, q * P:(q + 1) * P], wout_sb[:, :],
                                      start=True, stop=True)
                        if q:
                            m.then_inc(f_done, 1)

            over_iterations(pe, body)

        @block.vector
        def _(dve):
            dve.wait_ge(weights_in, 16 * N_WEIGHTS)
            dve.wait_ge(const_act, 1)
            dve.tensor_scalar(a_neg[:, :, :], a_exp[:, :, :], -1.0, None, ALU.mult).then_inc(const_dve, 1)
            dve.wait_ge(const_pool, 3)
            for k in range(KD):
                for c in range(TAPS):
                    dve.tensor_scalar(conv_diag[:, k, c, :], ident[:, :], conv_w_sb[:, k, c:c + 1], None, ALU.mult)
            for k in range(HH):
                dve.tensor_scalar(w2_diag[:, k, :], ident2[:, :], w2_sb[:, k:k + 1], None, ALU.mult)
            dve.memset(gT[M:M + 1, :], 1.0)
            dve.scalar_tensor_tensor(b1f[:, :], w1_sb[:, :], bin_sb[:, 0:1], b1_sb[:, :], ALU.mult, ALU.add)\
               .then_inc(const_dve, 1)

            def body(it, st):
                tile_a, tile_b, half, tile_p, tile_f = it, it - 1, it - LAG_SCAN, it - LAG_POST, it - LAG_FFN
                for s in range(SLOTS):
                    i, d = s // KD, s % KD
                    if st["scan"]:
                        slot = half * SLOTS + s
                        chunk = half // 2
                        hb = i % 2
                        if d == 0:
                            wait(dve, hT_done, (half * HALF + i - 1) * 4)
                            if i == 0:
                                wait(dve, state_saved, half * HALF - HALF)
                        dve.wait_ge(decay_ready, slot + 1)
                        dve.wait_ge(inp_ready, slot + 1)
                        dve.tensor_tensor_scan(h[:, hb, d, :], decay[:, s % RING, :], inp[:, s % RING, :],
                                               state[:, chunk % 2, (half * HALF + i) % NS, d:d + 1],
                                               ALU.mult, ALU.add).then_inc(scan_done, 1)
                    if adds(s, st, i, None):
                        step = half * HALF + i - 1
                        idx = step * 4 + d
                        dve.wait_ge(hT_done, idx + 1)
                        if s >= KD and s < 2 * KD:
                            dve.wait_ge(acc_init, (half // 2) * 4 + 4)
                        wait(dve, acc_done, idx - 3)
                        y = acc[:, bass.ds((step // NS % 2) * 4 + d, 1), :].rearrange("p o d -> p (o d)")
                        dve.scalar_tensor_tensor(y, hT_bank[d % 2][:, :], c_tok[:, step % (3 * NS), d:d + 1], y,
                                                 ALU.mult, ALU.add).then_inc(acc_done, 1)
                    if st["scan"] and d == KD - 1:
                        dve.wait_ge(scan_done, half * SLOTS + s + 1)
                        dve.tensor_scalar(state[:, 1, (half * HALF + i) % NS, :], h[:, hb, :, TC - 1], 1.0, None, ALU.mult).then_inc(state_saved, 1)
                    if st["prep_a"] and s == 3:
                        dve.wait_ge(x_in, 16 * tile_a + 16)
                        for q in range(SUB):
                            o = dve.bn_stats(x_stats[:, q, :], xt[:, q, :])
                        dve.drain()
                        for q in range(SUB):
                            o = dve.bn_aggr(x_mv[:, q, :], x_stats[:, q, :])
                        dve.drain()
                        slot8 = tile_a % 8
                        dve.tensor_scalar(x_norm[:, slot8, 0:2], x_mv[:, :, 0], 1.0, None, ALU.mult)
                        dve.tensor_scalar(x_norm[:, slot8, 2:4], x_mv[:, :, 1], EPS, None, ALU.add)
                        dve.tensor_scalar(x_norm[:, slot8, 4:6], x_mv[:, :, 1], 1.0 + EPS, EPS * EPS, ALU.mult, ALU.add)\
                           .then_inc(x_step, 1)
                    if st["prep_a"] and s == 6:
                        dve.wait_ge(x_rstd, tile_a + 1)
                        wait(dve, xT_done, tile_a)
                        slot8 = tile_a % 8
                        for q in range(SUB):
                            o = dve.tensor_scalar(xn[:, q, :], xt[:, q, :], x_norm[:, slot8, q:q + 1],
                                                  x_norm[:, slot8, 4 + q:5 + q], ALU.subtract, ALU.mult)
                        o.then_inc(xn_ready, 1)
                    if st["prep_b"] and s in (4, 8):
                        q = (s == 8)
                        dve.wait_ge(e_ready, 2 * tile_b + 1 + q)
                        dve.tensor_scalar(e_sb[:, :, :], e_sb[:, :, :], EXP_CAP, None, ALU.min).then_inc(e_capped, 1)
                    if st["prep_b"] and s in (6, 10):
                        q = (s == 10)
                        dve.wait_ge(l_ready, 2 * tile_b + 1 + q)
                        if q == 0:
                            if st["scan"]:
                                wait(dve, decay_ready, (tile_b - 2) // 2 * (2 * SLOTS))
                        bnk = (lo_bank, hi_bank)[q]
                        for k in range(2):
                            o = dve.scalar_tensor_tensor(
                                dt_sb[:, tile_b // 2 % 2, 2 * q + k, bass.ds((tile_b % 2) * TT, TT)],
                                bnk[:, k * TT:(k + 1) * TT], b_dt_sb[:, 2 * q + k:2 * q + k + 1], e_sb[:, k, :],
                                ALU.add, ALU.max)
                        o.then_inc(dt_ready, 1)
                    if st["post"] and s == 23:
                        dve.wait_ge(xr_in, 16 * tile_p + 16)
                        slot8 = tile_p % 8
                        for q in range(SUB):
                            o = dve.tensor_scalar(xl[:, q, :], xr[:, q, :], x_norm[:, slot8, q:q + 1],
                                                  x_norm[:, slot8, 2 + q:3 + q], ALU.subtract, ALU.mult)
                        o.then_inc(r_step, 1)
                        dve.wait_ge(r_step, 3 * tile_p + 1)
                        dve.wait_ge(proj_done, tile_p + 1)
                        dve.tensor_tensor(r_sb[:, :, :], post_bank[:, :].rearrange("p (q m) -> p q m", q=SUB), xl[:, :, :],
                                          ALU.add).then_inc(r_step, 1)
                    if st["post"] and s == 24:
                        dve.wait_ge(r_step, 3 * tile_p + 2)
                        for q in range(SUB):
                            o = dve.bn_stats(r_stats[:, q, :], r_sb[:, q, :])
                        dve.drain()
                        for q in range(SUB):
                            o = dve.bn_aggr(r_mv[:, q, :], r_stats[:, q, :])
                        dve.drain()
                        dve.tensor_scalar(r_std[:, 0, :], r_mv[:, :, 1], EPS, None, ALU.add).then_inc(r_step, 1)
                    if st["post"] and s == 26:
                        dve.wait_ge(r_rstd, tile_p + 1)
                        wait(dve, x1_ready, tile_p)
                        for q in range(SUB):
                            o = dve.tensor_scalar(rn[:, q, :], r_sb[:, q, :], r_mv[:, q, 0:1], r_std[:, 1, q:q + 1],
                                                  ALU.subtract, ALU.mult)
                        o.then_inc(rn_ready, 1)
                    if st["post"] and s == 28:
                        dve.wait_ge(x1_ready, tile_p + 1)
                        for q in range(SUB):
                            o = dve.bn_stats(x1_stats[:, q, :], x1[:, tile_p % 2, q, :])
                        dve.drain()
                        for q in range(SUB):
                            o = dve.bn_aggr(x1_mv[:, q, :], x1_stats[:, q, :])
                        dve.drain()
                        dve.tensor_scalar(x1_std[:, 0, :], x1_mv[:, :, 1], EPS, None, ALU.add).then_inc(x1_step, 1)
                    if st["post"] and s == 30:
                        dve.wait_ge(x1_rstd, tile_p + 1)
                        wait(dve, x1T_done, tile_p)
                        for q in range(SUB):
                            o = dve.tensor_scalar(x1n[:, q, :], x1[:, tile_p % 2, q, :], x1_mv[:, q, 0:1],
                                                  x1_std[:, 1, q:q + 1], ALU.subtract, ALU.mult)
                        o.then_inc(x1n_ready, 1)
                    if st["ffn"] and s == 15:
                        dve.wait_ge(f_done, tile_f + 1)
                        for q in range(SUB):
                            o = dve.bn_stats(f_stats[:, q, :], ffn_bank[:, q * DM:(q + 1) * DM])
                        dve.drain()
                        for q in range(SUB):
                            o = dve.bn_aggr(f_mv[:, q, :], f_stats[:, q, :])
                        dve.drain()
                        dve.tensor_scalar(f_std[:, 0, :], f_mv[:, :, 1], EPS, None, ALU.add).then_inc(f_step, 1)
                    if st["ffn"] and s == 17:
                        dve.wait_ge(f_rstd, tile_f + 1)
                        wait(dve, fo_ready, tile_f)
                        dve.scalar_tensor_tensor(f_shift[:, :], f_mv[:, :, 0], -1.0, f_std[:, 1, :], ALU.mult, ALU.mult)\
                           .then_inc(f_shifted, 1)

            over_iterations(dve, body)


N_WEIGHTS = 24

_INS = ["x", "w_in", "conv_w", "conv_b", "w_xproj", "w_dt", "b_dt", "A_log", "D", "w_out", "ln_g", "ln_b"]
_FFN = ["Win", "bin_", "W1", "b1", "W2", "b2", "Wout", "bout"]


def kernel(**inputs):
    import numpy as _np
    import concourse.bacc as _bacc
    from concourse import mybir as _mybir
    from concourse.bass_utils import run_bass_kernel_spmd as _run

    nc = _bacc.Bacc("TRN2", target_bir_lowering=False, num_devices=1)
    arrays, args = {}, []
    for name in ["L0_attn_" + n for n in _INS] + ["L0_ffn_" + n for n in _FFN]:
        a = _np.ascontiguousarray(inputs[name])
        arrays[f"in_{name}_dram"] = a
        args.append(nc.dram_tensor(f"in_{name}_dram", a.shape, _mybir.dt.from_np(a.dtype), kind="ExternalInput").ap())
    shape = inputs["L0_attn_x"].shape
    args.append(nc.dram_tensor("out_0_dram", shape, _mybir.dt.float32, kind="ExternalOutput").ap())
    bass_mamba_mlp_sandwich(nc, *args)
    r = _run(nc, [arrays], core_ids=[0])
    return r.results[0]["out_0_dram"]
```

```python
from contextlib import ExitStack

import concourse.bass as bass
from concourse import mybir

F32 = mybir.dt.float32
ALU = mybir.AluOpType
ACT = mybir.ActivationFunctionType

P = 128
B, L, DM = 16, 1024, 256
DI, NS, TAPS = 512, 16, 4
KM, KD = DM // P, DI // P
TT, TC = 256, 512
SUB = TT // P
TILES = B * L // TT
HALF = 8
SLOTS = HALF * KD
M, INNER = 64, 16
HH = INNER // 2
EPS = 1e-5
EXP_CAP = 2.0 ** 60
RING = 8
ROWS = 4
LAG_B, LAG_SCAN, LAG_POST, LAG_FFN = 1, 3, 5, 6


def bass_mamba_mlp_sandwich(nc, x, w_in, conv_w, conv_b, w_xproj, w_dt, b_dt, A_log, D, w_out,
                            ln_g, ln_b, Win, bin_, W1, b1, W2, b2, Wout, bout, out):
    with ExitStack() as ctx:
        def sb(name, *shape):
            return ctx.enter_context(nc.sbuf_tensor(name, list(shape), F32))

        def sem(name):
            return ctx.enter_context(nc.semaphore(name))

        b_rows = nc.dram_tensor("b_rows", [TILES, NS, TT], F32).ap()
        gates = nc.dram_tensor("gates", [TILES, P, SUB * DI], F32).ap()

        w_in_sb = sb("w_in_sb", P, KM, 2 * DI)
        w_dt_sb = sb("w_dt_sb", P, KD, DI)
        w_x_sb = sb("w_x_sb", P, KD, 2 * NS)
        w_out_sb = sb("w_out_sb", P, KD, DM)
        conv_w_sb = sb("conv_w_sb", P, KD, TAPS)
        conv_diag = sb("conv_diag", P, KD, TAPS, P)
        conv_b_sb = sb("conv_b_sb", P, KD)
        b_dt_sb = sb("b_dt_sb", P, KD)
        a_log_sb = sb("a_log_sb", P, KD, NS)
        a_exp = sb("a_exp", P, NS, KD)
        a_neg = sb("a_neg", P, NS, KD)
        d_sb = sb("d_sb", P, KD)
        g_sb = sb("g_sb", P, KM)
        beta_sb = sb("beta_sb", P, KM)
        win_sb = sb("win_sb", P, KM, 2 * M)
        bin_sb = sb("bin_sb", P, 1)
        w1_sb = sb("w1_sb", P, HH)
        b1_sb = sb("b1_sb", P, HH)
        b1f = sb("b1f", P, HH)
        w2_sb = sb("w2_sb", P, HH)
        w2_diag = sb("w2_diag", P, HH, M)
        b2_sb = sb("b2_sb", M, 1)
        wout_sb = sb("wout_sb", M + 1, DM)
        ident = sb("ident", P, P)
        ident2 = sb("ident2", P, M)
        minus_half = sb("minus_half", P, 4)

        xt = sb("xt", P, SUB, DM)
        x_stats = sb("x_stats", P, SUB, 6)
        x_mv = sb("x_mv", P, SUB, 2)
        x_norm = sb("x_norm", P, 8, 6)
        xn = sb("xn", P, SUB, DM)
        xnT = sb("xnT", P, KM, TT)
        xraw = sb("xraw", P, KD, TAPS - 1 + TT)
        tails = sb("tails", P, 5, KD, TAPS - 1)
        xb = sb("xb", P, KD, TT)
        xbD = sb("xbD", P, KD, TT)
        gate_w = sb("gate_w", P, SUB, DI)
        b_tok = sb("b_tok", P, SUB, P)
        b_rowsT = sb("b_rowsT", NS, TT)
        e_sb = sb("e_sb", P, 2, TT)

        dt_sb = sb("dt_sb", P, 2, KD, TC)
        u_sb = sb("u_sb", P, 2, KD, TC)
        c_tok = sb("c_tok", P, 3 * NS, 2 * SUB)
        acc = sb("acc", P, 4 * SUB, DI)
        b_bc = sb("b_bc", P, ROWS, TC)
        decay = sb("decay", P, RING, TC)
        inp = sb("inp", P, RING, TC)
        h = sb("h", P, 2, KD, TC)
        state = sb("state", P, 2, NS, KD)

        gate_r = sb("gate_r", P, SUB, DI)
        xr = sb("xr", P, SUB, DM)
        yg = sb("yg", P, SUB, DI)
        ygT = sb("ygT", P, SUB, KD, P)
        xl = sb("xl", P, SUB, DM)
        r_sb = sb("r_sb", P, SUB, DM)
        r_stats = sb("r_stats", P, SUB, 6)
        r_mv = sb("r_mv", P, SUB, 2)
        r_std = sb("r_std", P, 2, SUB)
        rn = sb("rn", P, SUB, DM)
        x1 = sb("x1", P, 2, SUB, DM)
        x1_stats = sb("x1_stats", P, SUB, 6)
        x1_mv = sb("x1_mv", P, SUB, 2)
        x1_std = sb("x1_std", P, 2, SUB)
        x1n = sb("x1n", P, SUB, DM)
        x1nT = sb("x1nT", P, KM, TT)
        hid = sb("hid", P, 2, TT)
        gT = sb("gT", M + 1, TT)
        f_stats = sb("f_stats", P, SUB, 6)
        f_mv = sb("f_mv", P, SUB, 2)
        f_std = sb("f_std", P, 2, SUB)
        f_shift = sb("f_shift", P, SUB)
        fo = sb("fo", P, SUB, DM)
        x2 = sb("x2", P, SUB, DM)

        def bank(name):
            return ctx.enter_context(nc.psum_tensor(name, [P, 512], F32))

        hT_bank = [bank("hT0"), bank("hT1")]
        lo_bank, hi_bank = bank("lo_bank"), bank("hi_bank")
        mix0, mix1 = bank("mix0"), bank("mix1")
        post_bank, ffn_bank = bank("post_bank"), bank("ffn_bank")

        weights_in = sem("weights_in")
        waits_taken = sem("waits_taken")
        const_pool = sem("const_pool")
        const_act = sem("const_act")
        const_dve = sem("const_dve")
        x_in = sem("x_in")
        x_step = sem("x_step")
        x_rstd = sem("x_rstd")
        xn_ready = sem("xn_ready")
        xT_done = sem("xT_done")
        xnT_ready = sem("xnT_ready")
        xh_done = sem("xh_done")
        xraw_ready = sem("xraw_ready")
        head_ready = sem("head_ready")
        tail_saved = sem("tail_saved")
        conv_done = sem("conv_done")
        z_done = sem("z_done")
        xb_ready = sem("xb_ready")
        gate_ready = sem("gate_ready")
        gate_stored = sem("gate_stored")
        bc_done = sem("bc_done")
        c_ready = sem("c_ready")
        bT_done = sem("bT_done")
        bT_ready = sem("bT_ready")
        b_stored = sem("b_stored")
        dt_mm = sem("dt_mm")
        e_ready = sem("e_ready")
        e_capped = sem("e_capped")
        l_ready = sem("l_ready")
        dt_ready = sem("dt_ready")
        u_ready = sem("u_ready")
        xbD_ready = sem("xbD_ready")
        xbDT_done = sem("xbDT_done")
        acc_init = sem("acc_init")
        b_bc_in = [sem(f"b_bc_in{i}") for i in range(ROWS)]
        decay_ready = sem("decay_ready")
        inp_ready = sem("inp_ready")
        scan_done = sem("scan_done")
        state_saved = sem("state_saved")
        hT_done = sem("hT_done")
        acc_done = sem("acc_done")
        gate_in = sem("gate_in")
        xr_in = sem("xr_in")
        yg_ready = sem("yg_ready")
        ygT_done = sem("ygT_done")
        ygT_ready = sem("ygT_ready")
        proj_done = sem("proj_done")
        r_step = sem("r_step")
        r_rstd = sem("r_rstd")
        rn_ready = sem("rn_ready")
        x1_ready = sem("x1_ready")
        x1_step = sem("x1_step")
        x1_rstd = sem("x1_rstd")
        x1n_ready = sem("x1n_ready")
        x1T_done = sem("x1T_done")
        x1nT_ready = sem("x1nT_ready")
        s_done = sem("s_done")
        hid_ready = sem("hid_ready")
        hid_used = sem("hid_used")
        gT_ready = sem("gT_ready")
        f_done = sem("f_done")
        f_step = sem("f_step")
        f_rstd = sem("f_rstd")
        f_shifted = sem("f_shifted")
        fo_ready = sem("fo_ready")
        x2_ready = sem("x2_ready")
        out_stored = sem("out_stored")

        def wait(eng, s, value):
            if not isinstance(value, int) or value > 0:
                eng.wait_ge(s, value)

        def take_waits(pool):
            pool.sem_inc(waits_taken, 1)

        x_tiles = x.rearrange("b (t s p) m -> (b t) p s m", p=P, s=SUB)
        out_tiles = out.rearrange("b (t s p) m -> (b t) p s m", p=P, s=SUB)

        n_it = TILES + LAG_FFN
        edges = sorted({0, LAG_B, LAG_B + 1, LAG_SCAN, LAG_SCAN + 1, LAG_POST, LAG_FFN, LAG_FFN + 1, TILES, TILES + LAG_B,
                        TILES + LAG_SCAN, TILES + LAG_SCAN + 1, TILES + LAG_POST, n_it})

        def over_iterations(eng, body):
            for lo, hi in zip(edges, edges[1:]):
                stages = {
                    "prep_a": lo < TILES,
                    "prep_b": LAG_B <= lo < TILES + LAG_B,
                    "scan": LAG_SCAN <= lo < TILES + LAG_SCAN,
                    "before": LAG_SCAN < lo < TILES + LAG_SCAN,
                    "drain": lo == TILES + LAG_SCAN,
                    "post": LAG_POST <= lo < TILES + LAG_POST,
                    "ffn": LAG_FFN <= lo,
                }
                if hi - lo == 1:
                    body(lo, stages)
                else:
                    with eng.Fori(lo, hi) as it:
                        body(it, stages)

        def adds(s, stages, i, before):
            return (stages["scan"] and (i > 0 or stages["before"])) or (stages["drain"] and i == 0)

        block = ctx.enter_context(nc.Block())

        @block.sync
        def _(sp):
            n_w = 0
            for dst, src in (
                (w_in_sb[:, :, :], w_in.rearrange("(k p) n -> p k n", p=P)),
                (w_dt_sb[:, :, :], w_dt.rearrange("(k p) n -> p k n", p=P)),
                (w_x_sb[:, :, :], w_xproj.rearrange("(k p) n -> p k n", p=P)),
                (w_out_sb[:, :, :], w_out.rearrange("(k p) n -> p k n", p=P)),
                (conv_w_sb[:, :, :], conv_w.rearrange("(k p) o c -> p k (o c)", p=P)),
                (conv_b_sb[:, :], conv_b.rearrange("(k p) -> p k", p=P)),
                (b_dt_sb[:, :], b_dt.rearrange("(k p) -> p k", p=P)),
                (a_log_sb[:, :, :], A_log.rearrange("(k p) n -> p k n", p=P)),
                (d_sb[:, :], D.rearrange("(k p) -> p k", p=P)),
                (g_sb[:, :], ln_g.rearrange("(k p) -> p k", p=P)),
                (beta_sb[:, :], ln_b.rearrange("(k p) -> p k", p=P)),
                (win_sb[:, :, 0:M], Win.rearrange("(k p) n -> p k n", p=P)),
                (win_sb[:, :, M:2 * M], Win.rearrange("(k p) n -> p k n", p=P)),
                (bin_sb[0:M, :], bin_.rearrange("(m o) -> m o", o=1)),
                (bin_sb[M:2 * M, :], bin_.rearrange("(m o) -> m o", o=1)),
                (w1_sb[0:M, :], W1[:, 0:HH]), (w1_sb[M:2 * M, :], W1[:, HH:INNER]),
                (b1_sb[0:M, :], b1[:, 0:HH]), (b1_sb[M:2 * M, :], b1[:, HH:INNER]),
                (w2_sb[0:M, :], W2[:, 0:HH]), (w2_sb[M:2 * M, :], W2[:, HH:INNER]),
                (b2_sb[:, :], b2.rearrange("(m o) -> m o", o=1)),
                (wout_sb[0:M, :], Wout),
                (wout_sb[M:M + 1, :], bout.rearrange("(o n) -> o n", o=1)),
            ):
                sp.dma_start(dst, src, allow_slow_non_contiguous=True).then_inc(weights_in, 16)
                n_w += 1
            assert n_w == N_WEIGHTS

            def body(it, st):
                tile_a, tile_b, half, tile_p, tile_f = it, it - 1, it - LAG_SCAN, it - LAG_POST, it - LAG_FFN
                for s in range(SLOTS):
                    i = s // KD
                    if st["prep_a"] and s == 0:
                        wait(sp, xn_ready, tile_a)
                        sp.dma_start(xt[:, :, :], x_tiles[tile_a]).then_inc(x_in, 16)
                    if st["scan"] and s % KD == 0:
                        n, chunk = (half * HALF + i) % NS, half // 2
                        wait(sp, inp_ready, half * SLOTS + (i - ROWS + 1) * KD)
                        if i == 0:
                            wait(sp, b_stored, chunk * 32 + 32)
                        rows = b_rows.rearrange("(c t) n k -> c n t k", t=2)[chunk, n]
                        sp.dma_start(b_bc[:, i % ROWS, :].rearrange("p (t k) -> p t k", t=2),
                                     rows.unsqueeze(0).broadcast_to([P, 2, TT])).then_inc(b_bc_in[i % ROWS], 16)
                    if st["post"] and s == 0:
                        wait(sp, gate_stored, tile_p * 16 + 16)
                        wait(sp, yg_ready, tile_p)
                        sp.dma_start(gate_r[:, :, :].rearrange("p s d -> p (s d)"), gates[tile_p]).then_inc(gate_in, 16)
                    if st["post"] and s == 8:
                        wait(sp, x1_ready, tile_p)
                        sp.dma_start(xr[:, :, :], x_tiles[tile_p]).then_inc(xr_in, 16)
                    if st["ffn"] and s == 31:
                        wait(sp, x2_ready, tile_f + 1)
                        sp.dma_start(out_tiles[tile_f], x2[:, :, :]).then_inc(out_stored, 16)
                    if st["prep_b"] and s == 9:
                        wait(sp, gate_ready, tile_b + 1)
                        sp.dma_start(gates[tile_b], gate_w[:, :, :].rearrange("p s d -> p (s d)")).then_inc(gate_stored, 16)
                    if st["prep_b"] and s == 15:
                        wait(sp, bT_ready, tile_b + 1)
                        sp.dma_start(b_rows[tile_b], b_rowsT[:, :]).then_inc(b_stored, 16)

            over_iterations(sp, body)
            sp.wait_ge(out_stored, TILES * 16)
            sp.wait_ge(gate_stored, TILES * 16)
            sp.wait_ge(b_stored, TILES * 16)

        @block.gpsimd
        def _(pool):
            pool.memset(ident[:, :], 0.0)
            pool.memset(ident2[:, :], 0.0)
            pool.memset(minus_half[:, :], -0.5)
            pool.memset(tails[:, 0, :, :], 0.0)
            pool.memset(state[:, 0, :, :], 0.0)
            pool.memset(b_tok[:, :, :], 0.0).then_inc(const_pool, 1)
            pool.wait_ge(const_pool, 1)
            pool.affine_select(out=ident[:, :], in_=ident[:, :], compare_op=ALU.not_equal, fill=1.0,
                               base=0, pattern=[[-1, P]], channel_multiplier=1)
            pool.affine_select(out=ident2[:, :], in_=ident2[:, :], compare_op=ALU.not_equal, fill=1.0,
                               base=0, pattern=[[-1, M]], channel_multiplier=1).then_inc(const_pool, 1)
            pool.wait_ge(const_pool, 2)
            pool.affine_select(out=ident2[:, :], in_=ident2[:, :], compare_op=ALU.not_equal, fill=1.0,
                               base=-M, pattern=[[-1, M]], channel_multiplier=1).then_inc(const_pool, 1)

            def body(it, st):
                tile_a, tile_b, half, tile_p, tile_f = it, it - 1, it - LAG_SCAN, it - LAG_POST, it - LAG_FFN
                for s in range(SLOTS):
                    i, d = s // KD, s % KD
                    if st["prep_a"] and s == 8:
                        pool.wait_ge(x_step, tile_a + 1)
                        v = x_norm[:, tile_a % 8, 2:6]
                        take_waits(pool)
                        pool.tensor_tensor(v, v, minus_half[:, :], ALU.pow).then_inc(x_rstd, 1)
                    if st["prep_a"] and s == 16:
                        wait(pool, conv_done, tile_a)
                        wait(pool, tail_saved, tile_a)
                        take_waits(pool)
                        pool.tensor_copy(xraw[:, :, 0:TAPS - 1], tails[:, tile_a % 4, :, :]).then_inc(head_ready, 1)
                    if st["prep_a"] and s == 22:
                        pool.wait_ge(xraw_ready, 2 * tile_a + 2)
                        pool.wait_ge(head_ready, tile_a + 1)
                        take_waits(pool)
                        pool.tensor_copy(tails[:, tile_a % 4 + 1, :, :], xraw[:, :, TT:TT + TAPS - 1]).then_inc(tail_saved, 1)
                    if st["prep_b"] and s in (13, 17):
                        q = (s == 17)
                        pool.wait_ge(dt_ready, 2 * tile_b + 1 + q)
                        pool.wait_ge(xb_ready, tile_b + 1)
                        if q == 0:
                            if st["scan"]:
                                wait(pool, inp_ready, (tile_b - 2) // 2 * (2 * SLOTS))
                        cols = slice(tile_b % 2 * TT, tile_b % 2 * TT + TT)
                        t0 = (tile_b % 2) * TT
                        take_waits(pool)
                        pool.tensor_tensor(u_sb[:, tile_b // 2 % 2, 2 * q:2 * q + 2, bass.ds(t0, TT)],
                                           dt_sb[:, tile_b // 2 % 2, 2 * q:2 * q + 2, bass.ds(t0, TT)],
                                           xb[:, 2 * q:2 * q + 2, :], ALU.mult).then_inc(u_ready, 1)
                    if st["post"] and s == 9:
                        pool.wait_ge(gate_in, 16 * tile_p + 16)
                        pool.wait_ge(acc_done, ((tile_p // 2) * NS + NS - 1) * 4 + (tile_p % 2) * SUB + SUB)
                        wait(pool, ygT_done, 2 * tile_p)
                        take_waits(pool)
                        pool.tensor_tensor(yg[:, :, :], acc[:, bass.ds((tile_p % 4) * SUB, SUB), :],
                                           gate_r[:, :, :], ALU.mult).then_inc(yg_ready, 1)
                    if st["post"] and s == 29:
                        pool.wait_ge(r_step, 3 * tile_p + 3)
                        pool.tensor_tensor(r_std[:, 1, :], r_std[:, 0, :], minus_half[:, 0:SUB], ALU.pow).then_inc(r_rstd, 1)
                    if st["post"] and s == 31:
                        pool.wait_ge(rn_ready, tile_p + 1)
                        pool.wait_ge(xr_in, 16 * tile_p + 16)
                        wait(pool, x2_ready, tile_p - 1)
                        take_waits(pool)
                        pool.tensor_tensor(x1[:, tile_p % 2, :, :], xr[:, :, :], rn[:, :, :], ALU.add).then_inc(x1_ready, 1)
                    if st["ffn"] and s == 1:
                        pool.wait_ge(x1_step, tile_f + 1)
                        pool.tensor_tensor(x1_std[:, 1, :], x1_std[:, 0, :], minus_half[:, 0:SUB], ALU.pow).then_inc(x1_rstd, 1)
                    if st["ffn"] and s == 19:
                        pool.wait_ge(f_step, tile_f + 1)
                        pool.tensor_tensor(f_std[:, 1, :], f_std[:, 0, :], minus_half[:, 0:SUB], ALU.pow).then_inc(f_rstd, 1)
                    if st["ffn"] and s == 22:
                        pool.wait_ge(fo_ready, tile_f + 1)
                        wait(pool, out_stored, 16 * tile_f)
                        take_waits(pool)
                        pool.tensor_tensor(x2[:, :, :], x1[:, tile_f % 2, :, :], fo[:, :, :], ALU.add).then_inc(x2_ready, 1)
                    if st["scan"]:
                        chunk = half // 2
                        if d == 0:
                            pool.wait_ge(b_bc_in[i % ROWS], (half * (HALF // ROWS) + i // ROWS) * 16 + 16)
                        if s == 0:
                            pool.wait_ge(u_ready, chunk * 4 + 4)
                        wait(pool, scan_done, half * SLOTS + s - RING + 1)
                        take_waits(pool)
                        pool.tensor_tensor(inp[:, s % RING, :], u_sb[:, chunk % 2, d, :], b_bc[:, i % ROWS, :],
                                           ALU.mult).then_inc(inp_ready, 1)

            over_iterations(pool, body)

        @block.scalar
        def _(act):
            act.wait_ge(weights_in, 16 * N_WEIGHTS)
            act.activation(a_exp[:, :, :].rearrange("p n k -> p k n"), a_log_sb[:, :, :], ACT.Exp).then_inc(const_act, 1)
            act.wait_ge(const_dve, 1)

            def body(it, st):
                tile_a, tile_b, half, tile_p, tile_f = it, it - 1, it - LAG_SCAN, it - LAG_POST, it - LAG_FFN
                for s in range(SLOTS):
                    i, d = s // KD, s % KD
                    if st["scan"]:
                        chunk = half // 2
                        if s == 0:
                            act.wait_ge(dt_ready, chunk * 4 + 4)
                        wait(act, scan_done, half * SLOTS + s - RING + 1)
                        act.activation(decay[:, s % RING, :], dt_sb[:, chunk % 2, d, :], ACT.Exp,
                                       scale=a_neg[:, (half * HALF + i) % NS, d:d + 1]).then_inc(decay_ready, 1)
                    if st["prep_b"] and s in (10, 14):
                        q = (s == 14)
                        act.wait_ge(dt_mm, 2 * tile_b + 1 + q)
                        wait(act, dt_ready, 2 * tile_b + q)
                        bnk = (lo_bank, hi_bank)[q]
                        for k in range(2):
                            a = act.activation(e_sb[:, k, :], bnk[:, k * TT:(k + 1) * TT], ACT.Exp,
                                               bias=b_dt_sb[:, 2 * q + k:2 * q + k + 1])
                        a.then_inc(e_ready, 1)
                    if st["prep_b"] and s in (11, 15):
                        q = (s == 15)
                        act.wait_ge(e_capped, 2 * tile_b + 1 + q)
                        act.activation(e_sb[:, :, :], e_sb[:, :, :], ACT.Ln, bias=1.0).then_inc(l_ready, 1)
                    if st["prep_b"] and s == 9:
                        act.wait_ge(xb_ready, tile_b + 1)
                        wait(act, xbDT_done, 2 * tile_b)
                        for k in range(KD):
                            a = act.activation(xbD[:, k, :], xb[:, k, :], ACT.Copy, scale=d_sb[:, k:k + 1])
                        a.then_inc(xbD_ready, 1)
                    if st["prep_b"] and s in (14, 15):
                        q = (s == 15)
                        act.wait_ge(xbDT_done, 2 * tile_b + 1 + q)
                        if st["scan"]:
                            wait(act, yg_ready, tile_b - 3)
                        act.activation(acc[:, bass.ds((tile_b % 4) * SUB + q, 1), :].rearrange("p o d -> p (o d)"),
                                       (mix0, mix1)[q][:, :], ACT.Copy).then_inc(acc_init, 1)
                    if st["prep_a"] and s == 16:
                        act.wait_ge(xT_done, tile_a + 1)
                        wait(act, z_done, tile_a)
                        for k in range(KM):
                            a = act.activation(xnT[:, k, :], mix0[:, k * TT:(k + 1) * TT], ACT.Identity,
                                               scale=g_sb[:, k:k + 1], bias=beta_sb[:, k:k + 1])
                        a.then_inc(xnT_ready, 1)
                    if st["prep_a"] and s in (19, 21):
                        q = (s == 21)
                        act.wait_ge(xh_done, 2 * tile_a + 1 + q)
                        wait(act, conv_done, tile_a)
                        wait(act, tail_saved, tile_a)
                        act.activation(xraw[:, 2 * q:2 * q + 2, TAPS - 1:],
                                       (mix1, mix0)[q][:, :].rearrange("p (k t) -> p k t", k=2), ACT.Copy)\
                           .then_inc(xraw_ready, 1)
                    if st["prep_b"] and s == 1:
                        act.wait_ge(conv_done, tile_b + 1)
                        wait(act, u_ready, 2 * tile_b)
                        wait(act, xbD_ready, tile_b)
                        wait(act, dt_mm, 2 * tile_b)
                        for k in range(KD):
                            a = act.activation(xb[:, k, :], (lo_bank, hi_bank)[k // 2][:, k % 2 * TT:k % 2 * TT + TT],
                                               ACT.Silu, bias=conv_b_sb[:, k:k + 1])
                        a.then_inc(xb_ready, 1)
                        act.wait_ge(z_done, tile_b + 1)
                        wait(act, gate_stored, 16 * tile_b)
                        for q in range(SUB):
                            a = act.activation(gate_w[:, q, :], (mix1, mix0)[q][:, :], ACT.Silu)
                        a.then_inc(gate_ready, 1)
                        act.preload_act_table_set("natural_log_exp_and_others")
                    if st["prep_b"] and s == 6:
                        act.wait_ge(bc_done, tile_b + 1)
                        if st["scan"]:
                            wait(act, acc_done, (tile_b - 4) // 2 * (NS * 4))
                        wait(act, bT_done, tile_b)
                        bc = mix0[:, 0:SUB * 2 * NS].rearrange("p (s n) -> p s n", s=SUB)
                        act.activation(b_tok[:, :, 0:NS], bc[:, :, 0:NS], ACT.Copy)
                        act.activation(c_tok[:, bass.ds((tile_b // 2 % 3) * NS, NS), bass.ds((tile_b % 2) * SUB, SUB)]
                                       .rearrange("p n s -> p s n"), bc[:, :, NS:2 * NS], ACT.Copy).then_inc(c_ready, 1)
                    if st["prep_b"] and s == 8:
                        act.wait_ge(bT_done, tile_b + 1)
                        wait(act, b_stored, 16 * tile_b)
                        act.activation(b_rowsT[:, :], mix0[0:NS, 0:TT], ACT.Copy).then_inc(bT_ready, 1)
                    if st["post"] and s in (16, 18):
                        q = (s == 18)
                        act.wait_ge(ygT_done, 2 * tile_p + 1 + q)
                        wait(act, proj_done, tile_p)
                        act.activation(ygT[:, q, :, :], post_bank[:, :].rearrange("p (k t) -> p k t", k=KD),
                                       ACT.Copy).then_inc(ygT_ready, 1)
                    if st["ffn"] and s == 4:
                        act.wait_ge(x1T_done, tile_f + 1)
                        wait(act, s_done, tile_f)
                        act.activation(x1nT[:, :, :], post_bank[:, :].rearrange("p (k t) -> p k t", k=KM),
                                       ACT.Copy).then_inc(x1nT_ready, 1)
                    if st["ffn"] and 6 <= s < 6 + HH:
                        k = s - 6
                        if k == 0:
                            act.wait_ge(s_done, tile_f + 1)
                        wait(act, hid_used, HH * tile_f + max(k - 1, 0))
                        act.activation(hid[:, k % 2, :], post_bank[:, 0:TT], ACT.Relu, scale=w1_sb[:, k:k + 1],
                                       bias=b1f[:, k:k + 1]).then_inc(hid_ready, 1)
                    if st["ffn"] and s == 15:
                        act.wait_ge(hid_used, HH * tile_f + HH)
                        wait(act, f_done, tile_f)
                        act.activation(gT[0:M, :], ffn_bank[0:M, 0:TT], ACT.Identity, bias=b2_sb[:, :]).then_inc(gT_ready, 1)
                    if st["ffn"] and s == 21:
                        act.wait_ge(f_shifted, tile_f + 1)
                        wait(act, x2_ready, tile_f)
                        for q in range(SUB):
                            a = act.activation(fo[:, q, :], ffn_bank[:, q * DM:(q + 1) * DM], ACT.Identity,
                                               scale=f_std[:, 1, q:q + 1], bias=f_shift[:, q:q + 1])
                        a.then_inc(fo_ready, 1)

            over_iterations(act, body)

        @block.tensor
        def _(pe):
            pe.wait_ge(weights_in, 16 * N_WEIGHTS)
            pe.wait_ge(const_pool, 3)
            pe.wait_ge(const_dve, 2)

            def transpose_to(out_ap, in_ap):
                return pe.transpose(out_ap, in_ap, ident[:, :])

            def body(it, st):
                tile_a, tile_b, half, tile_p, tile_f = it, it - 1, it - LAG_SCAN, it - LAG_POST, it - LAG_FFN
                for s in range(SLOTS):
                    i, d = s // KD, s % KD
                    if adds(s, st, i, None):
                        step = half * HALF + i - 1
                        idx = step * 4 + d
                        if d == 0:
                            pe.wait_ge(scan_done, (step + 1) * KD)
                        wait(pe, acc_done, idx - 1)
                        bnk = hT_bank[d % 2]
                        hb = (i - 1) % 2
                        for k in range(KD):
                            t = transpose_to(bnk[:, k * P:(k + 1) * P], h[:, hb, k, d * P:(d + 1) * P])
                        t.then_inc(hT_done, 1)
                    if st["prep_b"] and 2 <= s < 2 + 2 * KD:
                        k, kk = (s - 2) // 2, s % 2
                        bnk = (lo_bank, hi_bank)[k // 2]
                        if s == 2:
                            pe.wait_ge(xb_ready, tile_b + 1)
                        for c in (2 * kk, 2 * kk + 1):
                            m = pe.matmul(bnk[:, k % 2 * TT:k % 2 * TT + TT], w_dt_sb[:, c, k * P:(k + 1) * P], xb[:, c, :],
                                          start=(c == 0), stop=(c == KD - 1))
                        if k % 2 and kk:
                            m.then_inc(dt_mm, 1)
                    if st["prep_b"] and s in (9, 10):
                        q = s - 9
                        if q == 0:
                            pe.wait_ge(xbD_ready, tile_b + 1)
                            pe.wait_ge(bT_ready, tile_b + 1)
                            pe.wait_ge(gate_ready, tile_b + 1)
                        for k in range(KD):
                            t = transpose_to((mix0, mix1)[q][:, k * P:(k + 1) * P], xbD[:, k, q * P:(q + 1) * P])
                        t.then_inc(xbDT_done, 1)
                    if st["prep_a"] and s == 11:
                        pe.wait_ge(xn_ready, tile_a + 1)
                        wait(pe, acc_init, 2 * (tile_a - 1) + 1)
                        for k in range(KM):
                            for q in range(SUB):
                                t = transpose_to(mix0[:, k * TT + q * P:k * TT + (q + 1) * P], xn[:, q, k * P:(k + 1) * P])
                        t.then_inc(xT_done, 1)
                    if st["prep_a"] and 13 <= s < 17:
                        k = s - 13
                        if k == 0:
                            pe.wait_ge(xnT_ready, tile_a + 1)
                            wait(pe, acc_init, 2 * tile_a)
                        bnk = (mix1, mix0)[k // 2]
                        for c in range(KM):
                            m = pe.matmul(bnk[:, k % 2 * TT:k % 2 * TT + TT], w_in_sb[:, c, k * P:(k + 1) * P], xnT[:, c, :],
                                          start=(c == 0), stop=(c == KM - 1))
                        if k % 2:
                            m.then_inc(xh_done, 1)
                    if st["prep_a"] and 21 <= s < 29:
                        k, kk = (s - 21) // 2, (s - 21) % 2
                        if s == 21:
                            pe.wait_ge(head_ready, tile_a + 1)
                            wait(pe, dt_ready, 2 * tile_a)
                        if k % 2 == 0 and kk == 0:
                            pe.wait_ge(xraw_ready, 2 * tile_a + 1 + k // 2)
                        bnk = (lo_bank, hi_bank)[k // 2]
                        for c in (2 * kk, 2 * kk + 1):
                            m = pe.matmul(bnk[:, k % 2 * TT:k % 2 * TT + TT], conv_diag[:, k, c, :], xraw[:, k, c:c + TT],
                                          start=(c == 0), stop=(c == TAPS - 1))
                        if s == 28:
                            m.then_inc(conv_done, 1)
                    if st["prep_a"] and 17 <= s < 21:
                        q, c = (s - 17) // 2, (s - 17) % 2
                        if c == 0:
                            pe.wait_ge(xraw_ready, 2 * tile_a + 1 + q)
                        m = pe.matmul((mix1, mix0)[q][:, :], xnT[:, c, q * P:(q + 1) * P], w_in_sb[:, c, DI:2 * DI],
                                      start=(c == 0), stop=(c == KM - 1))
                        if s == 20:
                            m.then_inc(z_done, 1)
                    if st["prep_b"] and s == 1:
                        pe.wait_ge(xb_ready, tile_b + 1)
                        pe.wait_ge(gate_ready, tile_b + 1)
                        for q in range(SUB):
                            for c in range(KD):
                                m = pe.matmul(mix0[:, q * 2 * NS:(q + 1) * 2 * NS], xb[:, c, q * P:(q + 1) * P], w_x_sb[:, c, :],
                                              start=(c == 0), stop=(c == KD - 1))
                        m.then_inc(bc_done, 1)
                    if st["prep_b"] and s == 3:
                        pe.wait_ge(c_ready, tile_b + 1)
                        for q in range(SUB):
                            t = transpose_to(mix0[:, q * P:(q + 1) * P], b_tok[:, q, :])
                        t.then_inc(bT_done, 1)
                    if st["post"] and s in (11, 13):
                        q = (s == 13)
                        if q == 0:
                            pe.wait_ge(yg_ready, tile_p + 1)
                            wait(pe, hid_ready, HH * (tile_p - 1) + HH)
                        else:
                            pe.wait_ge(ygT_ready, 2 * tile_p + 1)
                        for k in range(KD):
                            t = transpose_to(post_bank[:, k * P:(k + 1) * P], yg[:, q, k * P:(k + 1) * P])
                        t.then_inc(ygT_done, 1)
                    if st["post"] and 15 <= s < 23:
                        q, c = (s - 15) // KD, (s - 15) % KD
                        if s == 15:
                            pe.wait_ge(ygT_ready, 2 * tile_p + 2)
                        m = pe.matmul(post_bank[:, q * DM:(q + 1) * DM], ygT[:, q, c, :], w_out_sb[:, c, :],
                                      start=(c == 0), stop=(c == KD - 1))
                        if s == 22:
                            m.then_inc(proj_done, 1)
                    if st["post"] and s == 31:
                        pe.wait_ge(x1n_ready, tile_p + 1)
                        pe.wait_ge(r_step, 3 * tile_p + 2)
                        for k in range(KM):
                            for q in range(SUB):
                                t = transpose_to(post_bank[:, k * TT + q * P:k * TT + (q + 1) * P], x1n[:, q, k * P:(k + 1) * P])
                        t.then_inc(x1T_done, 1)
                    if st["ffn"] and s == 1:
                        pe.wait_ge(x1nT_ready, tile_f + 1)
                        for c in range(KM):
                            m = pe.matmul(post_bank[:, 0:TT], win_sb[:, c, :], x1nT[:, c, :], start=(c == 0), stop=(c == KM - 1))
                        m.then_inc(s_done, 1)
                    if st["ffn"] and 3 <= s < 3 + HH:
                        k = s - 3
                        pe.wait_ge(hid_ready, HH * tile_f + k + 1)
                        if k == 0:
                            wait(pe, fo_ready, tile_f)
                        pe.matmul(ffn_bank[0:M, 0:TT], w2_diag[:, k, :], hid[:, k % 2, :], start=(k == 0),
                                  stop=(k == HH - 1)).then_inc(hid_used, 1)
                    if st["ffn"] and s in (12, 13):
                        q = s - 12
                        if q == 0:
                            pe.wait_ge(gT_ready, tile_f + 1)
                        m = pe.matmul(ffn_bank[:, q * DM:(q + 1) * DM], gT[:, q * P:(q + 1) * P], wout_sb[:, :],
                                      start=True, stop=True)
                        if q:
                            m.then_inc(f_done, 1)

            over_iterations(pe, body)

        @block.vector
        def _(dve):
            dve.wait_ge(weights_in, 16 * N_WEIGHTS)
            dve.wait_ge(const_act, 1)
            dve.tensor_scalar(a_neg[:, :, :], a_exp[:, :, :], -1.0, None, ALU.mult).then_inc(const_dve, 1)
            dve.wait_ge(const_pool, 3)
            for k in range(KD):
                for c in range(TAPS):
                    dve.tensor_scalar(conv_diag[:, k, c, :], ident[:, :], conv_w_sb[:, k, c:c + 1], None, ALU.mult)
            for k in range(HH):
                dve.tensor_scalar(w2_diag[:, k, :], ident2[:, :], w2_sb[:, k:k + 1], None, ALU.mult)
            dve.memset(gT[M:M + 1, :], 1.0)
            dve.scalar_tensor_tensor(b1f[:, :], w1_sb[:, :], bin_sb[:, 0:1], b1_sb[:, :], ALU.mult, ALU.add)\
               .then_inc(const_dve, 1)

            def body(it, st):
                tile_a, tile_b, half, tile_p, tile_f = it, it - 1, it - LAG_SCAN, it - LAG_POST, it - LAG_FFN
                for s in range(SLOTS):
                    i, d = s // KD, s % KD
                    if st["scan"]:
                        slot = half * SLOTS + s
                        chunk = half // 2
                        hb = i % 2
                        if d == 0:
                            wait(dve, hT_done, (half * HALF + i - 1) * 4)
                            if i == 0:
                                wait(dve, state_saved, half * HALF - HALF)
                        dve.wait_ge(decay_ready, slot + 1)
                        dve.wait_ge(inp_ready, slot + 1)
                        dve.tensor_tensor_scan(h[:, hb, d, :], decay[:, s % RING, :], inp[:, s % RING, :],
                                               state[:, chunk % 2, (half * HALF + i) % NS, d:d + 1],
                                               ALU.mult, ALU.add).then_inc(scan_done, 1)
                    if adds(s, st, i, None):
                        step = half * HALF + i - 1
                        idx = step * 4 + d
                        dve.wait_ge(hT_done, idx + 1)
                        if s >= KD and s < 2 * KD:
                            dve.wait_ge(acc_init, (half // 2) * 4 + 4)
                        wait(dve, acc_done, idx - 3)
                        y = acc[:, bass.ds((step // NS % 2) * 4 + d, 1), :].rearrange("p o d -> p (o d)")
                        dve.scalar_tensor_tensor(y, hT_bank[d % 2][:, :], c_tok[:, step % (3 * NS), d:d + 1], y,
                                                 ALU.mult, ALU.add).then_inc(acc_done, 1)
                    if st["scan"] and d == KD - 1:
                        dve.wait_ge(scan_done, half * SLOTS + s + 1)
                        dve.tensor_scalar(state[:, 1, (half * HALF + i) % NS, :], h[:, hb, :, TC - 1], 1.0, None, ALU.mult).then_inc(state_saved, 1)
                    if st["prep_a"] and s == 3:
                        dve.wait_ge(x_in, 16 * tile_a + 16)
                        for q in range(SUB):
                            o = dve.bn_stats(x_stats[:, q, :], xt[:, q, :])
                        dve.drain()
                        for q in range(SUB):
                            o = dve.bn_aggr(x_mv[:, q, :], x_stats[:, q, :])
                        dve.drain()
                        slot8 = tile_a % 8
                        dve.tensor_scalar(x_norm[:, slot8, 0:2], x_mv[:, :, 0], 1.0, None, ALU.mult)
                        dve.tensor_scalar(x_norm[:, slot8, 2:4], x_mv[:, :, 1], EPS, None, ALU.add)
                        dve.tensor_scalar(x_norm[:, slot8, 4:6], x_mv[:, :, 1], 1.0 + EPS, EPS * EPS, ALU.mult, ALU.add)\
                           .then_inc(x_step, 1)
                    if st["prep_a"] and s == 6:
                        dve.wait_ge(x_rstd, tile_a + 1)
                        wait(dve, xT_done, tile_a)
                        slot8 = tile_a % 8
                        for q in range(SUB):
                            o = dve.tensor_scalar(xn[:, q, :], xt[:, q, :], x_norm[:, slot8, q:q + 1],
                                                  x_norm[:, slot8, 4 + q:5 + q], ALU.subtract, ALU.mult)
                        o.then_inc(xn_ready, 1)
                    if st["prep_b"] and s in (6, 10):
                        q = (s == 10)
                        dve.wait_ge(e_ready, 2 * tile_b + 1 + q)
                        dve.tensor_scalar(e_sb[:, :, :], e_sb[:, :, :], EXP_CAP, None, ALU.min).then_inc(e_capped, 1)
                    if st["prep_b"] and s in (8, 12):
                        q = (s == 12)
                        dve.wait_ge(l_ready, 2 * tile_b + 1 + q)
                        if q == 0:
                            if st["scan"]:
                                wait(dve, decay_ready, (tile_b - 2) // 2 * (2 * SLOTS))
                        bnk = (lo_bank, hi_bank)[q]
                        for k in range(2):
                            o = dve.scalar_tensor_tensor(
                                dt_sb[:, tile_b // 2 % 2, 2 * q + k, bass.ds((tile_b % 2) * TT, TT)],
                                bnk[:, k * TT:(k + 1) * TT], b_dt_sb[:, 2 * q + k:2 * q + k + 1], e_sb[:, k, :],
                                ALU.add, ALU.max)
                        o.then_inc(dt_ready, 1)
                    if st["post"] and s == 23:
                        dve.wait_ge(xr_in, 16 * tile_p + 16)
                        slot8 = tile_p % 8
                        for q in range(SUB):
                            o = dve.tensor_scalar(xl[:, q, :], xr[:, q, :], x_norm[:, slot8, q:q + 1],
                                                  x_norm[:, slot8, 2 + q:3 + q], ALU.subtract, ALU.mult)
                        o.then_inc(r_step, 1)
                        dve.wait_ge(r_step, 3 * tile_p + 1)
                        dve.wait_ge(proj_done, tile_p + 1)
                        dve.tensor_tensor(r_sb[:, :, :], post_bank[:, :].rearrange("p (q m) -> p q m", q=SUB), xl[:, :, :],
                                          ALU.add).then_inc(r_step, 1)
                    if st["post"] and s == 24:
                        dve.wait_ge(r_step, 3 * tile_p + 2)
                        for q in range(SUB):
                            o = dve.bn_stats(r_stats[:, q, :], r_sb[:, q, :])
                        dve.drain()
                        for q in range(SUB):
                            o = dve.bn_aggr(r_mv[:, q, :], r_stats[:, q, :])
                        dve.drain()
                        dve.tensor_scalar(r_std[:, 0, :], r_mv[:, :, 1], EPS, None, ALU.add).then_inc(r_step, 1)
                    if st["post"] and s == 26:
                        dve.wait_ge(r_rstd, tile_p + 1)
                        wait(dve, x1_ready, tile_p)
                        for q in range(SUB):
                            o = dve.tensor_scalar(rn[:, q, :], r_sb[:, q, :], r_mv[:, q, 0:1], r_std[:, 1, q:q + 1],
                                                  ALU.subtract, ALU.mult)
                        o.then_inc(rn_ready, 1)
                    if st["post"] and s == 28:
                        dve.wait_ge(x1_ready, tile_p + 1)
                        for q in range(SUB):
                            o = dve.bn_stats(x1_stats[:, q, :], x1[:, tile_p % 2, q, :])
                        dve.drain()
                        for q in range(SUB):
                            o = dve.bn_aggr(x1_mv[:, q, :], x1_stats[:, q, :])
                        dve.drain()
                        dve.tensor_scalar(x1_std[:, 0, :], x1_mv[:, :, 1], EPS, None, ALU.add).then_inc(x1_step, 1)
                    if st["post"] and s == 30:
                        dve.wait_ge(x1_rstd, tile_p + 1)
                        wait(dve, x1T_done, tile_p)
                        for q in range(SUB):
                            o = dve.tensor_scalar(x1n[:, q, :], x1[:, tile_p % 2, q, :], x1_mv[:, q, 0:1],
                                                  x1_std[:, 1, q:q + 1], ALU.subtract, ALU.mult)
                        o.then_inc(x1n_ready, 1)
                    if st["ffn"] and s == 14:
                        dve.wait_ge(f_done, tile_f + 1)
                        for q in range(SUB):
                            o = dve.bn_stats(f_stats[:, q, :], ffn_bank[:, q * DM:(q + 1) * DM])
                        dve.drain()
                        for q in range(SUB):
                            o = dve.bn_aggr(f_mv[:, q, :], f_stats[:, q, :])
                        dve.drain()
                        dve.tensor_scalar(f_std[:, 0, :], f_mv[:, :, 1], EPS, None, ALU.add).then_inc(f_step, 1)
                    if st["ffn"] and s == 16:
                        dve.wait_ge(f_rstd, tile_f + 1)
                        wait(dve, fo_ready, tile_f)
                        dve.scalar_tensor_tensor(f_shift[:, :], f_mv[:, :, 0], -1.0, f_std[:, 1, :], ALU.mult, ALU.mult)\
                           .then_inc(f_shifted, 1)

            over_iterations(dve, body)


N_WEIGHTS = 24

_INS = ["x", "w_in", "conv_w", "conv_b", "w_xproj", "w_dt", "b_dt", "A_log", "D", "w_out", "ln_g", "ln_b"]
_FFN = ["Win", "bin_", "W1", "b1", "W2", "b2", "Wout", "bout"]


def kernel(**inputs):
    import numpy as _np
    import concourse.bacc as _bacc
    from concourse import mybir as _mybir
    from concourse.bass_utils import run_bass_kernel_spmd as _run

    nc = _bacc.Bacc("TRN2", target_bir_lowering=False, num_devices=1)
    arrays, args = {}, []
    for name in ["L0_attn_" + n for n in _INS] + ["L0_ffn_" + n for n in _FFN]:
        a = _np.ascontiguousarray(inputs[name])
        arrays[f"in_{name}_dram"] = a
        args.append(nc.dram_tensor(f"in_{name}_dram", a.shape, _mybir.dt.from_np(a.dtype), kind="ExternalInput").ap())
    shape = inputs["L0_attn_x"].shape
    args.append(nc.dram_tensor("out_0_dram", shape, _mybir.dt.float32, kind="ExternalOutput").ap())
    bass_mamba_mlp_sandwich(nc, *args)
    r = _run(nc, [arrays], core_ids=[0])
    return r.results[0]["out_0_dram"]
```

```python
from contextlib import ExitStack

import concourse.bass as bass
from concourse import mybir

F32 = mybir.dt.float32
ALU = mybir.AluOpType
ACT = mybir.ActivationFunctionType

P = 128
B, L, DM = 16, 1024, 256
DI, NS, TAPS = 512, 16, 4
KM, KD = DM // P, DI // P
TT, TC = 256, 512
SUB = TT // P
TILES = B * L // TT
HALF = 8
SLOTS = HALF * KD
M, INNER = 64, 16
HH = INNER // 2
EPS = 1e-5
EXP_CAP = 2.0 ** 60
RING = 8
PAIR = 2
HID = 4
ROWS = 4
DT_AT = (0, 0, 1, 1, 3, 4, 5, 6, 7, 9, 9, 11, 12, 12, 13, 14)
BC_AT = (2, 2, 3, 3)
XH_AT = (15, 15, 16, 16, 19, 20, 21, 22)
CONV_AT = (20, 20, 21, 23, 23, 24, 24, 25, 25, 26, 26, 27, 27, 28, 29, 29)
Z_AT = (21, 22, 28, 30)
PROJ_AT = (15, 16, 17, 17, 18, 18, 19, 19)
UNROLL = 3
LAG_B, LAG_SCAN, LAG_POST, LAG_FFN, LAG_STORE = 1, 3, 5, 6, 7


def at(slots, s):
    return [j for j, slot in enumerate(slots) if slot == s]


def bass_mamba_mlp_sandwich(nc, x, w_in, conv_w, conv_b, w_xproj, w_dt, b_dt, A_log, D, w_out,
                            ln_g, ln_b, Win, bin_, W1, b1, W2, b2, Wout, bout, out):
    with ExitStack() as ctx:
        def sb(name, *shape):
            return ctx.enter_context(nc.sbuf_tensor(name, list(shape), F32))

        def sem(name):
            return ctx.enter_context(nc.semaphore(name))

        b_rows = nc.dram_tensor("b_rows", [TILES, NS, TT], F32).ap()
        gates = nc.dram_tensor("gates", [TILES, P, SUB * DI], F32).ap()

        w_in_sb = sb("w_in_sb", P, KM, 2 * DI)
        w_dt_sb = sb("w_dt_sb", P, KD, DI)
        w_x_sb = sb("w_x_sb", P, KD, 2 * NS)
        w_out_sb = sb("w_out_sb", P, KD, DM)
        conv_w_sb = sb("conv_w_sb", P, KD, TAPS)
        conv_diag = sb("conv_diag", P, KD, TAPS, P)
        conv_b_sb = sb("conv_b_sb", P, KD)
        b_dt_sb = sb("b_dt_sb", P, KD)
        a_log_sb = sb("a_log_sb", P, KD, NS)
        a_exp = sb("a_exp", P, NS, KD)
        a_neg = sb("a_neg", P, NS, KD)
        d_sb = sb("d_sb", P, KD)
        g_sb = sb("g_sb", P, KM)
        beta_sb = sb("beta_sb", P, KM)
        win_sb = sb("win_sb", P, KM, 2 * M)
        bin_sb = sb("bin_sb", P, 1)
        w1_sb = sb("w1_sb", P, HH)
        b1_sb = sb("b1_sb", P, HH)
        b1f = sb("b1f", P, HH)
        w2_sb = sb("w2_sb", P, HH)
        w2_diag = sb("w2_diag", P, HH, M)
        b2_sb = sb("b2_sb", M, 1)
        wout_sb = sb("wout_sb", M + 1, DM)
        ident = sb("ident", P, P)
        ident2 = sb("ident2", P, M)
        minus_half = sb("minus_half", P, 4)

        xt = sb("xt", P, SUB, DM)
        x_stats = sb("x_stats", P, SUB, 6)
        x_mv = sb("x_mv", P, SUB, 2)
        x_norm = sb("x_norm", P, 8, 6)
        x_shift = sb("x_shift", P, SUB)
        r_shift = sb("r_shift", P, SUB)
        xn = sb("xn", P, SUB, DM)
        xnT = sb("xnT", P, KM, TT)
        xraw = sb("xraw", P, KD, TAPS - 1 + TT)
        tails = sb("tails", P, 5, KD, TAPS - 1)
        xb = sb("xb", P, KD, TT)
        xbD = sb("xbD", P, KD, TT)
        gate_w = sb("gate_w", P, SUB, DI)
        bc_rows = sb("bc_rows", 2 * NS, TT)
        e_sb = sb("e_sb", P, 2, TT)

        dt_sb = sb("dt_sb", P, 2, KD, TC)
        u_sb = sb("u_sb", P, 2, KD, TC)
        c_tok = sb("c_tok", P, 3 * NS, 2 * SUB)
        acc = sb("acc", P, 4 * SUB, DI)
        b_bc = sb("b_bc", P, ROWS, TC)
        decay = sb("decay", P, RING // PAIR, PAIR, 1 + TC)
        inp = sb("inp", P, RING // PAIR, PAIR, 1 + TC)
        h = sb("h", P, 2, KD, 1 + TC)
        state = sb("state", P, 2, NS, KD)

        gate_r = sb("gate_r", P, SUB, DI)
        xr = sb("xr", P, SUB, DM)
        yg = sb("yg", P, SUB, DI)
        ygT = sb("ygT", P, SUB, KD, P)
        xm = sb("xm", P, SUB, DM)
        r_sb = sb("r_sb", P, SUB, DM)
        r_stats = sb("r_stats", P, SUB, 6)
        r_mv = sb("r_mv", P, SUB, 2)
        r_std = sb("r_std", P, 2, SUB)
        rn = sb("rn", P, SUB, DM)
        x1 = sb("x1", P, 2, SUB, DM)
        x1_stats = sb("x1_stats", P, SUB, 6)
        x1_mv = sb("x1_mv", P, SUB, 2)
        x1_std = sb("x1_std", P, 2, SUB)
        x1n = sb("x1n", P, SUB, DM)
        x1nT = sb("x1nT", P, KM, TT)
        hid = sb("hid", P, HID, TT)
        gT = sb("gT", M + 1, TT)
        f_stats = sb("f_stats", P, SUB, 6)
        f_mv = sb("f_mv", P, SUB, 2)
        f_std = sb("f_std", P, 2, SUB)
        f_shift = sb("f_shift", P, SUB)
        fo = sb("fo", P, SUB, DM)
        x2 = sb("x2", P, SUB, DM)

        def bank(name):
            return ctx.enter_context(nc.psum_tensor(name, [P, 512], F32))

        hT_bank = [bank("hT0"), bank("hT1")]
        lo_bank, hi_bank = bank("lo_bank"), bank("hi_bank")
        mix0, mix1 = bank("mix0"), bank("mix1")
        post_bank, ffn_bank = bank("post_bank"), bank("ffn_bank")

        weights_in = sem("weights_in")
        waits_taken = sem("waits_taken")
        dve_waits_taken = sem("dve_waits_taken")
        pe_waits_taken = sem("pe_waits_taken")
        const_pool = sem("const_pool")
        const_act = sem("const_act")
        const_dve = sem("const_dve")
        x_in = sem("x_in")
        x_stats_done = sem("x_stats_done")
        x_mv_done = sem("x_mv_done")
        r_stats_done = sem("r_stats_done")
        r_mv_done = sem("r_mv_done")
        x1_stats_done = sem("x1_stats_done")
        x1_mv_done = sem("x1_mv_done")
        f_stats_done = sem("f_stats_done")
        f_mv_done = sem("f_mv_done")
        xm_ready = sem("xm_ready")
        x_step = sem("x_step")
        x_rstd = sem("x_rstd")
        x_shifted = sem("x_shifted")
        r_shifted = sem("r_shifted")
        xn_ready = sem("xn_ready")
        xT_done = sem("xT_done")
        xnT_ready = sem("xnT_ready")
        xh_done = sem("xh_done")
        xraw_ready = sem("xraw_ready")
        head_ready = sem("head_ready")
        tail_saved = sem("tail_saved")
        conv_done = sem("conv_done")
        z_done = sem("z_done")
        xb_ready = sem("xb_ready")
        gate_ready = sem("gate_ready")
        gate_stored = sem("gate_stored")
        bc_done = sem("bc_done")
        c_ready = sem("c_ready")
        bc_rows_ready = sem("bc_rows_ready")
        cT_done = sem("cT_done")
        b_stored = sem("b_stored")
        dt_mm = sem("dt_mm")
        e_ready = sem("e_ready")
        e_capped = sem("e_capped")
        l_ready = sem("l_ready")
        dt_ready = sem("dt_ready")
        u_ready = sem("u_ready")
        xbD_ready = sem("xbD_ready")
        xbDT_done = sem("xbDT_done")
        acc_init = sem("acc_init")
        b_bc_in = [sem(f"b_bc_in{i}") for i in range(ROWS)]
        decay_ready = sem("decay_ready")
        inp_ready = sem("inp_ready")
        scan_done = sem("scan_done")
        first_ready = sem("first_ready")
        state_saved = sem("state_saved")
        hT_done = sem("hT_done")
        acc_done = sem("acc_done")
        gate_in = sem("gate_in")
        xr_in = sem("xr_in")
        yg_ready = sem("yg_ready")
        ygT_done = sem("ygT_done")
        ygT_ready = sem("ygT_ready")
        proj_done = sem("proj_done")
        r_step = sem("r_step")
        r_rstd = sem("r_rstd")
        rn_ready = sem("rn_ready")
        x1_ready = sem("x1_ready")
        x1_step = sem("x1_step")
        x1_rstd = sem("x1_rstd")
        x1n_ready = sem("x1n_ready")
        x1T_done = sem("x1T_done")
        x1nT_ready = sem("x1nT_ready")
        s_done = sem("s_done")
        hid_ready = sem("hid_ready")
        hid_used = sem("hid_used")
        gT_ready = sem("gT_ready")
        f_done = sem("f_done")
        f_step = sem("f_step")
        f_rstd = sem("f_rstd")
        f_shifted = sem("f_shifted")
        fo_ready = sem("fo_ready")
        x2_ready = sem("x2_ready")
        out_stored = sem("out_stored")

        def wait(eng, s, value):
            if not isinstance(value, int) or value > 0:
                eng.wait_ge(s, value)

        def take_waits(pool):
            pool.sem_inc(waits_taken, 1)

        x_tiles = x.rearrange("b (t s p) m -> (b t) p s m", p=P, s=SUB)
        out_tiles = out.rearrange("b (t s p) m -> (b t) p s m", p=P, s=SUB)

        n_it = TILES + LAG_STORE
        edges = sorted({-1, 0, LAG_B, LAG_B + 1, LAG_SCAN, LAG_SCAN + 1, LAG_POST, LAG_FFN, LAG_STORE, LAG_STORE + 1,
                        TILES - 1, TILES, TILES + LAG_B, TILES + LAG_SCAN, TILES + LAG_SCAN + 1, TILES + LAG_POST,
                        TILES + LAG_FFN, n_it})

        def over_iterations(eng, body):
            for lo, hi in zip(edges, edges[1:]):
                stages = {
                    "next_x": lo + 1 < TILES,
                    "prep_a": 0 <= lo < TILES,
                    "prep_b": LAG_B <= lo < TILES + LAG_B,
                    "scan": LAG_SCAN <= lo < TILES + LAG_SCAN,
                    "before": LAG_SCAN < lo < TILES + LAG_SCAN,
                    "drain": lo == TILES + LAG_SCAN,
                    "post": LAG_POST <= lo < TILES + LAG_POST,
                    "ffn": LAG_FFN <= lo < TILES + LAG_FFN,
                    "store": LAG_STORE <= lo,
                }
                peeled = (hi - lo) % UNROLL
                for it in range(lo, lo + peeled):
                    body(it, stages)
                if hi - lo > peeled:
                    with eng.Fori(0, (hi - lo) // UNROLL) as group:
                        for u in range(UNROLL):
                            body(group * UNROLL + (lo + peeled + u), stages)

        def adds(stages, i):
            return (stages["scan"] and (i > 0 or stages["before"])) or (stages["drain"] and i == 0)

        block = ctx.enter_context(nc.Block())

        @block.sync
        def _(sp):
            n_w = 0
            for dst, src in (
                (w_in_sb[:, :, :], w_in.rearrange("(k p) n -> p k n", p=P)),
                (w_dt_sb[:, :, :], w_dt.rearrange("(k p) n -> p k n", p=P)),
                (w_x_sb[:, :, :], w_xproj.rearrange("(k p) n -> p k n", p=P)),
                (w_out_sb[:, :, :], w_out.rearrange("(k p) n -> p k n", p=P)),
                (conv_w_sb[:, :, :], conv_w.rearrange("(k p) o c -> p k (o c)", p=P)),
                (conv_b_sb[:, :], conv_b.rearrange("(k p) -> p k", p=P)),
                (b_dt_sb[:, :], b_dt.rearrange("(k p) -> p k", p=P)),
                (a_log_sb[:, :, :], A_log.rearrange("(k p) n -> p k n", p=P)),
                (d_sb[:, :], D.rearrange("(k p) -> p k", p=P)),
                (g_sb[:, :], ln_g.rearrange("(k p) -> p k", p=P)),
                (beta_sb[:, :], ln_b.rearrange("(k p) -> p k", p=P)),
                (win_sb[:, :, 0:M], Win.rearrange("(k p) n -> p k n", p=P)),
                (win_sb[:, :, M:2 * M], Win.rearrange("(k p) n -> p k n", p=P)),
                (bin_sb[0:M, :], bin_.rearrange("(m o) -> m o", o=1)),
                (bin_sb[M:2 * M, :], bin_.rearrange("(m o) -> m o", o=1)),
                (w1_sb[0:M, :], W1[:, 0:HH]), (w1_sb[M:2 * M, :], W1[:, HH:INNER]),
                (b1_sb[0:M, :], b1[:, 0:HH]), (b1_sb[M:2 * M, :], b1[:, HH:INNER]),
                (w2_sb[0:M, :], W2[:, 0:HH]), (w2_sb[M:2 * M, :], W2[:, HH:INNER]),
                (b2_sb[:, :], b2.rearrange("(m o) -> m o", o=1)),
                (wout_sb[0:M, :], Wout),
                (wout_sb[M:M + 1, :], bout.rearrange("(o n) -> o n", o=1)),
            ):
                sp.dma_start(dst, src, allow_slow_non_contiguous=True).then_inc(weights_in, 16)
                n_w += 1
            assert n_w == N_WEIGHTS

            def body(it, st):
                tile_x, tile_a, tile_b, half = it + 1, it, it - LAG_B, it - LAG_SCAN
                tile_p, tile_f, tile_o = it - LAG_POST, it - LAG_FFN, it - LAG_STORE
                for s in range(SLOTS):
                    i = s // KD
                    if st["next_x"] and s == 12:
                        wait(sp, xn_ready, tile_x)
                        sp.dma_start(xt[:, :, :], x_tiles[tile_x]).then_inc(x_in, 16)
                    if st["scan"] and s % KD == 0:
                        n, chunk = (half * HALF + i) % NS, half // 2
                        wait(sp, inp_ready, half * SLOTS + (i - ROWS + 1) * KD)
                        if i == 0:
                            wait(sp, b_stored, chunk * 32 + 32)
                        rows = b_rows.rearrange("(c t) n k -> c n t k", t=2)[chunk, n]
                        sp.dma_start(b_bc[:, i % ROWS, :].rearrange("p (t k) -> p t k", t=2),
                                     rows.unsqueeze(0).broadcast_to([P, 2, TT])).then_inc(b_bc_in[i % ROWS], 16)
                    if st["post"] and s == 0:
                        wait(sp, gate_stored, tile_p * 16 + 16)
                        wait(sp, yg_ready, tile_p)
                        sp.dma_start(gate_r[:, :, :].rearrange("p s d -> p (s d)"), gates[tile_p]).then_inc(gate_in, 16)
                    if st["post"] and s == 12:
                        wait(sp, x1_ready, tile_p)
                        sp.dma_start(xr[:, :, :], x_tiles[tile_p]).then_inc(xr_in, 16)
                    if st["store"] and s == 14:
                        wait(sp, x2_ready, tile_o + 1)
                        sp.dma_start(out_tiles[tile_o], x2[:, :, :]).then_inc(out_stored, 16)
                    if st["prep_b"] and s == 15:
                        wait(sp, gate_ready, tile_b + 1)
                        sp.dma_start(gates[tile_b], gate_w[:, :, :].rearrange("p s d -> p (s d)")).then_inc(gate_stored, 16)
                    if st["prep_b"] and s == 20:
                        wait(sp, bc_rows_ready, tile_b + 1)
                        sp.dma_start(b_rows[tile_b], bc_rows[0:NS, :]).then_inc(b_stored, 16)

            over_iterations(sp, body)
            sp.wait_ge(out_stored, TILES * 16)
            sp.wait_ge(gate_stored, TILES * 16)
            sp.wait_ge(b_stored, TILES * 16)

        @block.gpsimd
        def _(pool):
            pool.memset(ident[:, :], 0.0)
            pool.memset(ident2[:, :], 0.0)
            pool.memset(minus_half[:, :], -0.5)
            pool.memset(decay[:, :, 1, 0:1], 0.0)
            pool.memset(tails[:, 0, :, :], 0.0)
            pool.memset(state[:, 0, :, :], 0.0).then_inc(const_pool, 1)
            pool.wait_ge(const_pool, 1)
            pool.affine_select(out=ident[:, :], in_=ident[:, :], compare_op=ALU.not_equal, fill=1.0,
                               base=0, pattern=[[-1, P]], channel_multiplier=1)
            pool.affine_select(out=ident2[:, :], in_=ident2[:, :], compare_op=ALU.not_equal, fill=1.0,
                               base=0, pattern=[[-1, M]], channel_multiplier=1).then_inc(const_pool, 1)
            pool.wait_ge(const_pool, 2)
            pool.affine_select(out=ident2[:, :], in_=ident2[:, :], compare_op=ALU.not_equal, fill=1.0,
                               base=-M, pattern=[[-1, M]], channel_multiplier=1).then_inc(const_pool, 1)

            def body(it, st):
                tile_x, tile_a, tile_b, half = it + 1, it, it - LAG_B, it - LAG_SCAN
                tile_p, tile_f, tile_o = it - LAG_POST, it - LAG_FFN, it - LAG_STORE
                for s in range(SLOTS):
                    i, d = s // KD, s % KD
                    if st["store"] and s == 3:
                        pool.wait_ge(fo_ready, tile_o + 1)
                        wait(pool, out_stored, 16 * tile_o)
                        take_waits(pool)
                        pool.tensor_tensor(x2[:, :, :], x1[:, tile_o % 2, :, :], fo[:, :, :], ALU.add).then_inc(x2_ready, 1)
                    if st["next_x"] and s == 12:
                        pool.wait_ge(x_step, tile_x + 1)
                        v = x_norm[:, tile_x % 8, 2:6]
                        take_waits(pool)
                        pool.tensor_tensor(v, v, minus_half[:, :], ALU.pow).then_inc(x_rstd, 1)
                    if st["prep_a"] and s == 15:
                        wait(pool, conv_done, tile_a)
                        wait(pool, tail_saved, tile_a)
                        take_waits(pool)
                        pool.tensor_copy(xraw[:, :, 0:TAPS - 1], tails[:, tile_a % 4, :, :]).then_inc(head_ready, 1)
                    if st["prep_a"] and s == 28:
                        pool.wait_ge(xraw_ready, 2 * tile_a + 2)
                        pool.wait_ge(head_ready, tile_a + 1)
                        take_waits(pool)
                        pool.tensor_copy(tails[:, tile_a % 4 + 1, :, :], xraw[:, :, TT:TT + TAPS - 1]).then_inc(tail_saved, 1)
                    if st["prep_b"] and s in (18, 23):
                        q = (s == 23)
                        pool.wait_ge(dt_ready, 2 * tile_b + 1 + q)
                        pool.wait_ge(xb_ready, tile_b + 1)
                        if q == 0:
                            if st["scan"]:
                                wait(pool, inp_ready, (tile_b - 2) // 2 * (2 * SLOTS))
                        t0 = (tile_b % 2) * TT
                        take_waits(pool)
                        pool.tensor_tensor(u_sb[:, tile_b // 2 % 2, 2 * q:2 * q + 2, bass.ds(t0, TT)],
                                           dt_sb[:, tile_b // 2 % 2, 2 * q:2 * q + 2, bass.ds(t0, TT)],
                                           xb[:, 2 * q:2 * q + 2, :], ALU.mult).then_inc(u_ready, 1)
                    if st["post"] and s == 10:
                        pool.wait_ge(gate_in, 16 * tile_p + 16)
                        pool.wait_ge(acc_done, ((tile_p // 2) * NS + NS - 1) * 4 + (tile_p % 2) * SUB + SUB)
                        wait(pool, ygT_done, 2 * tile_p)
                        take_waits(pool)
                        pool.tensor_tensor(yg[:, :, :], acc[:, bass.ds((tile_p % 4) * SUB, SUB), :],
                                           gate_r[:, :, :], ALU.mult).then_inc(yg_ready, 1)
                    if st["post"] and s == 26:
                        pool.wait_ge(r_step, 2 * tile_p + 2)
                        pool.tensor_tensor(r_std[:, 1, :], r_std[:, 0, :], minus_half[:, 0:SUB], ALU.pow).then_inc(r_rstd, 1)
                    if st["post"] and s == 28:
                        pool.wait_ge(rn_ready, tile_p + 1)
                        pool.wait_ge(xr_in, 16 * tile_p + 16)
                        wait(pool, x2_ready, tile_p - 1)
                        take_waits(pool)
                        pool.tensor_tensor(x1[:, tile_p % 2, :, :], xr[:, :, :], rn[:, :, :], ALU.add).then_inc(x1_ready, 1)
                    if st["post"] and s == 31:
                        pool.wait_ge(x1_step, tile_p + 1)
                        pool.tensor_tensor(x1_std[:, 1, :], x1_std[:, 0, :], minus_half[:, 0:SUB], ALU.pow).then_inc(x1_rstd, 1)
                    if st["ffn"] and s == 21:
                        pool.wait_ge(f_step, tile_f + 1)
                        pool.tensor_tensor(f_std[:, 1, :], f_std[:, 0, :], minus_half[:, 0:SUB], ALU.pow).then_inc(f_rstd, 1)
                    if st["scan"]:
                        chunk = half // 2
                        if d == 0:
                            pool.wait_ge(b_bc_in[i % ROWS], (half * (HALF // ROWS) + i // ROWS) * 16 + 16)
                        if s == 0:
                            pool.wait_ge(u_ready, chunk * 4 + 4)
                        if s % PAIR == 0:
                            wait(pool, scan_done, half * SLOTS + s - RING + PAIR)
                            take_waits(pool)
                            pool.tensor_tensor(inp[:, s // PAIR % (RING // PAIR), :, 1:], u_sb[:, chunk % 2, d:d + PAIR, :],
                                               b_bc[:, i % ROWS, :].unsqueeze(1).broadcast_to([P, PAIR, TC]),
                                               ALU.mult).then_inc(inp_ready, PAIR)

            over_iterations(pool, body)

        @block.scalar
        def _(act):
            act.wait_ge(weights_in, 16 * N_WEIGHTS)
            act.activation(a_exp[:, :, :].rearrange("p n k -> p k n"), a_log_sb[:, :, :], ACT.Exp).then_inc(const_act, 1)
            act.wait_ge(const_dve, 1)

            def body(it, st):
                tile_x, tile_a, tile_b, half = it + 1, it, it - LAG_B, it - LAG_SCAN
                tile_p, tile_f, tile_o = it - LAG_POST, it - LAG_FFN, it - LAG_STORE
                for s in range(SLOTS):
                    i, d = s // KD, s % KD
                    if st["scan"]:
                        chunk = half // 2
                        if s == 0:
                            act.wait_ge(dt_ready, chunk * 4 + 4)
                        pair = s // PAIR % (RING // PAIR)
                        if s % PAIR == 0:
                            wait(act, scan_done, half * SLOTS + s - RING + PAIR)
                        else:
                            wait(act, state_saved, half * HALF + i + 1 - NS)
                            act.activation(inp[:, pair, 1, 0:1], state[:, chunk % 2, (half * HALF + i) % NS, d:d + 1],
                                           ACT.Copy).then_inc(first_ready, 1)
                        act.activation(decay[:, pair, s % PAIR, 1:], dt_sb[:, chunk % 2, d, :], ACT.Exp,
                                       scale=a_neg[:, (half * HALF + i) % NS, d:d + 1]).then_inc(decay_ready, 1)
                    if st["prep_b"] and s in (14, 19):
                        q = (s == 19)
                        act.wait_ge(dt_mm, 2 * tile_b + 1 + q)
                        wait(act, dt_ready, 2 * tile_b + q)
                        bnk = (lo_bank, hi_bank)[q]
                        for k in range(2):
                            a = act.activation(e_sb[:, k, :], bnk[:, k * TT:(k + 1) * TT], ACT.Exp,
                                               bias=b_dt_sb[:, 2 * q + k:2 * q + k + 1])
                        a.then_inc(e_ready, 1)
                    if st["prep_b"] and s in (16, 21):
                        q = (s == 21)
                        act.wait_ge(e_capped, 2 * tile_b + 1 + q)
                        act.activation(e_sb[:, :, :], e_sb[:, :, :], ACT.Ln, bias=1.0).then_inc(l_ready, 1)
                    if st["prep_b"] and s == 7:
                        act.wait_ge(xb_ready, tile_b + 1)
                        wait(act, xbDT_done, 2 * tile_b)
                        for k in range(KD):
                            a = act.activation(xbD[:, k, :], xb[:, k, :], ACT.Copy, scale=d_sb[:, k:k + 1])
                        a.then_inc(xbD_ready, 1)
                    if st["prep_b"] and s in (13, 15):
                        q = (s == 13)
                        act.wait_ge(xbDT_done, 2 * tile_b + 2 - q)
                        if st["scan"]:
                            wait(act, yg_ready, tile_b - 3)
                        act.activation(acc[:, bass.ds((tile_b % 4) * SUB + q, 1), :].rearrange("p o d -> p (o d)"),
                                       (mix0, mix1)[q][:, :], ACT.Copy).then_inc(acc_init, 1)
                    if st["next_x"] and s == 17:
                        act.wait_ge(x_shifted, tile_x + 1)
                        wait(act, xT_done, tile_x)
                        for q in range(SUB):
                            a = act.activation(xn[:, q, :], xt[:, q, :], ACT.Identity,
                                               scale=x_norm[:, tile_x % 8, 4 + q:5 + q], bias=x_shift[:, q:q + 1])
                        a.then_inc(xn_ready, 1)
                    if st["prep_a"] and s == 12:
                        act.wait_ge(xT_done, tile_a + 1)
                        wait(act, z_done, tile_a)
                        for k in range(KM):
                            a = act.activation(xnT[:, k, :], mix0[:, k * TT:(k + 1) * TT], ACT.Identity,
                                               scale=g_sb[:, k:k + 1], bias=beta_sb[:, k:k + 1])
                        a.then_inc(xnT_ready, 1)
                    if st["prep_a"] and s in (21, 27):
                        q = (s == 27)
                        act.wait_ge(xh_done, 2 * tile_a + 1 + q)
                        wait(act, conv_done, tile_a)
                        wait(act, tail_saved, tile_a)
                        act.activation(xraw[:, 2 * q:2 * q + 2, TAPS - 1:],
                                       (mix1, mix0)[q][:, :].rearrange("p (k t) -> p k t", k=2), ACT.Copy)\
                           .then_inc(xraw_ready, 1)
                    if st["prep_b"] and s == 2:
                        act.preload_act_table_set("silu_and_others")
                        act.wait_ge(conv_done, tile_b + 1)
                        wait(act, u_ready, 2 * tile_b)
                        wait(act, xbD_ready, tile_b)
                        wait(act, dt_mm, 2 * tile_b)
                        for k in range(KD):
                            a = act.activation(xb[:, k, :], (lo_bank, hi_bank)[k // 2][:, k % 2 * TT:k % 2 * TT + TT],
                                               ACT.Silu, bias=conv_b_sb[:, k:k + 1])
                        a.then_inc(xb_ready, 1)
                        act.wait_ge(z_done, tile_b + 1)
                        wait(act, gate_stored, 16 * tile_b)
                        for q in range(SUB):
                            a = act.activation(gate_w[:, q, :], (mix1, mix0)[q][:, :], ACT.Silu)
                        a.then_inc(gate_ready, 1)
                        act.preload_act_table_set("natural_log_exp_and_others")
                    if st["ffn"] and s == 2:
                        act.wait_ge(x1T_done, tile_f + 1)
                        act.activation(x1nT[:, :, :], post_bank[:, :].rearrange("p (k t) -> p k t", k=KM),
                                       ACT.Copy).then_inc(x1nT_ready, 1)
                    if st["prep_b"] and s == 8:
                        act.wait_ge(bc_done, tile_b + 1)
                        wait(act, b_stored, 16 * tile_b)
                        wait(act, cT_done, tile_b)
                        act.activation(bc_rows[:, :], mix0[0:2 * NS, 0:TT], ACT.Copy).then_inc(bc_rows_ready, 1)
                    if st["prep_b"] and s == 10:
                        act.wait_ge(cT_done, tile_b + 1)
                        if st["scan"]:
                            wait(act, acc_done, (tile_b - 4) // 2 * (NS * 4))
                        act.activation(c_tok[:, bass.ds((tile_b // 2 % 3) * NS, NS), bass.ds((tile_b % 2) * SUB, SUB)]
                                       .rearrange("p n s -> p s n"),
                                       mix0[:, 0:SUB * 2 * NS].rearrange("p (s n) -> p s n", s=SUB)[:, :, NS:2 * NS],
                                       ACT.Copy).then_inc(c_ready, 1)
                    if st["post"] and s in (16, 18):
                        q = (s == 18)
                        act.wait_ge(ygT_done, 2 * tile_p + 1 + q)
                        wait(act, proj_done, tile_p)
                        act.activation(ygT[:, q, :, :], post_bank[:, :].rearrange("p (k t) -> p k t", k=KD),
                                       ACT.Copy).then_inc(ygT_ready, 1)
                    if st["post"] and s == 23:
                        act.wait_ge(xr_in, 16 * tile_p + 16)
                        wait(act, r_step, 2 * tile_p - 1)
                        for q in range(SUB):
                            a = act.activation(xm[:, q, :], xr[:, q, :], ACT.Identity, bias=x_norm[:, tile_p % 8, q:q + 1])
                        a.then_inc(xm_ready, 1)
                    if st["post"] and s == 28:
                        act.wait_ge(r_shifted, tile_p + 1)
                        wait(act, x1_ready, tile_p)
                        for q in range(SUB):
                            a = act.activation(rn[:, q, :], r_sb[:, q, :], ACT.Identity, scale=r_std[:, 1, q:q + 1],
                                               bias=r_shift[:, q:q + 1])
                        a.then_inc(rn_ready, 1)
                    if st["ffn"] and 7 <= s < 7 + HH:
                        k = s - 7
                        if k == 0:
                            act.wait_ge(s_done, tile_f + 1)
                        wait(act, hid_used, HH * tile_f + max(k - HID + 1, 0))
                        act.activation(hid[:, k % HID, :], post_bank[:, 0:TT], ACT.Relu, scale=w1_sb[:, k:k + 1],
                                       bias=b1f[:, k:k + 1]).then_inc(hid_ready, 1)
                    if st["ffn"] and s == 16:
                        act.wait_ge(hid_used, HH * tile_f + HH)
                        wait(act, f_done, tile_f)
                        act.activation(gT[0:M, :], ffn_bank[0:M, 0:TT], ACT.Identity, bias=b2_sb[:, :]).then_inc(gT_ready, 1)
                    if st["ffn"] and s == 25:
                        act.wait_ge(f_shifted, tile_f + 1)
                        wait(act, x2_ready, tile_f)
                        for q in range(SUB):
                            a = act.activation(fo[:, q, :], ffn_bank[:, q * DM:(q + 1) * DM], ACT.Identity,
                                               scale=f_std[:, 1, q:q + 1], bias=f_shift[:, q:q + 1])
                        a.then_inc(fo_ready, 1)

            over_iterations(act, body)

        @block.tensor
        def _(pe):
            pe.wait_ge(weights_in, 16 * N_WEIGHTS)
            pe.wait_ge(const_pool, 3)
            pe.wait_ge(const_dve, 2)

            def transpose_to(out_ap, in_ap):
                return pe.transpose(out_ap, in_ap, ident[:, :])

            def body(it, st):
                tile_x, tile_a, tile_b, half = it + 1, it, it - LAG_B, it - LAG_SCAN
                tile_p, tile_f, tile_o = it - LAG_POST, it - LAG_FFN, it - LAG_STORE
                for s in range(SLOTS):
                    i, d = s // KD, s % KD
                    if adds(st, i):
                        step = half * HALF + i - 1
                        idx = step * 4 + d
                        if d == 0:
                            pe.wait_ge(scan_done, (step + 1) * KD)
                        wait(pe, acc_done, idx - 1)
                        bnk = hT_bank[d % 2]
                        hb = (i - 1) % 2
                        for k in range(KD):
                            t = transpose_to(bnk[:, k * P:(k + 1) * P], h[:, hb, k, 1 + d * P:1 + (d + 1) * P])
                        t.then_inc(hT_done, 1)
                    if st["prep_b"]:
                        for j in at(DT_AT, s):
                            k, c = j // KD, j % KD
                            if j == 0:
                                pe.wait_ge(xb_ready, tile_b + 1)
                            m = pe.matmul((lo_bank, hi_bank)[k // 2][:, k % 2 * TT:k % 2 * TT + TT],
                                          w_dt_sb[:, c, k * P:(k + 1) * P], xb[:, c, :], start=(c == 0), stop=(c == KD - 1))
                            if k % 2 and c == KD - 1:
                                m.then_inc(dt_mm, 1)
                    if st["prep_b"] and s in (8, 10):
                        q = (s == 8)
                        if q:
                            pe.wait_ge(xbD_ready, tile_b + 1)
                            pe.wait_ge(gate_ready, tile_b + 1)
                        else:
                            pe.wait_ge(c_ready, tile_b + 1)
                            if st["prep_a"]:
                                pe.wait_ge(xnT_ready, tile_a + 1)
                        for k in range(KD):
                            t = transpose_to((mix0, mix1)[q][:, k * P:(k + 1) * P], xbD[:, k, q * P:(q + 1) * P])
                        t.then_inc(xbDT_done, 1)
                    if st["prep_a"] and s == 7:
                        pe.wait_ge(xn_ready, tile_a + 1)
                        wait(pe, c_ready, tile_a)
                        for k in range(KM):
                            for q in range(SUB):
                                t = transpose_to(mix0[:, k * TT + q * P:k * TT + (q + 1) * P], xn[:, q, k * P:(k + 1) * P])
                        t.then_inc(xT_done, 1)
                    if st["prep_a"]:
                        for j in at(XH_AT, s):
                            k, c = j // KM, j % KM
                            if j == 0:
                                pe.wait_ge(xnT_ready, tile_a + 1)
                            if j % KD == 0:
                                wait(pe, acc_init, 2 * tile_a - 1 + k // 2)
                            m = pe.matmul((mix1, mix0)[k // 2][:, k % 2 * TT:k % 2 * TT + TT],
                                          w_in_sb[:, c, k * P:(k + 1) * P], xnT[:, c, :], start=(c == 0), stop=(c == KM - 1))
                            if k % 2 and c == KM - 1:
                                m.then_inc(xh_done, 1)
                        for j in at(CONV_AT, s):
                            k, c = j // TAPS, j % TAPS
                            if j == 0:
                                pe.wait_ge(head_ready, tile_a + 1)
                                wait(pe, dt_ready, 2 * tile_a)
                            if c == 0 and k % 2 == 0:
                                pe.wait_ge(xraw_ready, 2 * tile_a + 1 + k // 2)
                            m = pe.matmul((lo_bank, hi_bank)[k // 2][:, k % 2 * TT:k % 2 * TT + TT],
                                          conv_diag[:, k, c, :], xraw[:, k, c:c + TT], start=(c == 0), stop=(c == TAPS - 1))
                            if j == len(CONV_AT) - 1:
                                m.then_inc(conv_done, 1)
                        for j in at(Z_AT, s):
                            q, c = j // KM, j % KM
                            if c == 0:
                                pe.wait_ge(xraw_ready, 2 * tile_a + 1 + q)
                            m = pe.matmul((mix1, mix0)[q][:, :], xnT[:, c, q * P:(q + 1) * P], w_in_sb[:, c, DI:2 * DI],
                                          start=(c == 0), stop=(c == KM - 1))
                            if j == len(Z_AT) - 1:
                                m.then_inc(z_done, 1)
                    if st["prep_b"]:
                        for c in at(BC_AT, s):
                            if c == 0:
                                pe.wait_ge(gate_ready, tile_b + 1)
                            m = pe.matmul(mix0[0:2 * NS, 0:TT], w_x_sb[:, c, :], xb[:, c, :], start=(c == 0), stop=(c == KD - 1))
                            if c == KD - 1:
                                m.then_inc(bc_done, 1)
                    if st["prep_b"] and s == 5:
                        pe.wait_ge(bc_rows_ready, tile_b + 1)
                        pe.sem_inc(pe_waits_taken, 1)
                        for q in range(SUB):
                            t = pe.transpose(mix0[:, q * 2 * NS:(q + 1) * 2 * NS], bc_rows[:, q * P:(q + 1) * P],
                                             ident[0:2 * NS, 0:2 * NS])
                        t.then_inc(cT_done, 1)
                    if st["post"] and s in (11, 13):
                        q = (s == 13)
                        if q == 0:
                            pe.wait_ge(yg_ready, tile_p + 1)
                            wait(pe, hid_ready, HH * tile_p)
                        else:
                            pe.wait_ge(ygT_ready, 2 * tile_p + 1)
                        for k in range(KD):
                            t = transpose_to(post_bank[:, k * P:(k + 1) * P], yg[:, q, k * P:(k + 1) * P])
                        t.then_inc(ygT_done, 1)
                    if st["post"]:
                        for j in at(PROJ_AT, s):
                            q, c = j // KD, j % KD
                            if j == 0:
                                pe.wait_ge(ygT_ready, 2 * tile_p + 2)
                            m = pe.matmul(post_bank[:, q * DM:(q + 1) * DM], ygT[:, q, c, :], w_out_sb[:, c, :],
                                          start=(c == 0), stop=(c == KD - 1))
                            if j == len(PROJ_AT) - 1:
                                m.then_inc(proj_done, 1)
                    if st["post"] and s == 31:
                        pe.wait_ge(x1n_ready, tile_p + 1)
                        pe.wait_ge(r_step, 2 * tile_p + 1)
                        for k in range(KM):
                            for q in range(SUB):
                                t = transpose_to(post_bank[:, k * TT + q * P:k * TT + (q + 1) * P], x1n[:, q, k * P:(k + 1) * P])
                        t.then_inc(x1T_done, 1)
                    if st["ffn"] and s in (1, 2):
                        c = s - 1
                        if c == 0:
                            pe.wait_ge(x1nT_ready, tile_f + 1)
                        m = pe.matmul(post_bank[:, 0:TT], win_sb[:, c, :], x1nT[:, c, :], start=(c == 0), stop=(c == KM - 1))
                        if c == KM - 1:
                            m.then_inc(s_done, 1)
                    if st["ffn"] and 4 <= s < 4 + HH:
                        k = s - 4
                        pe.wait_ge(hid_ready, HH * tile_f + k + 1)
                        if k == 0:
                            wait(pe, fo_ready, tile_f)
                        pe.matmul(ffn_bank[0:M, 0:TT], w2_diag[:, k, :], hid[:, k % HID, :], start=(k == 0),
                                  stop=(k == HH - 1)).then_inc(hid_used, 1)
                    if st["ffn"] and s in (13, 14):
                        q = s - 13
                        if q == 0:
                            pe.wait_ge(gT_ready, tile_f + 1)
                        m = pe.matmul(ffn_bank[:, q * DM:(q + 1) * DM], gT[:, q * P:(q + 1) * P], wout_sb[:, :],
                                      start=True, stop=True)
                        if q:
                            m.then_inc(f_done, 1)

            over_iterations(pe, body)

        @block.vector
        def _(dve):
            dve.wait_ge(weights_in, 16 * N_WEIGHTS)
            dve.wait_ge(const_act, 1)
            dve.tensor_scalar(a_neg[:, :, :], a_exp[:, :, :], -1.0, None, ALU.mult).then_inc(const_dve, 1)
            dve.wait_ge(const_pool, 3)
            for k in range(KD):
                for c in range(TAPS):
                    dve.tensor_scalar(conv_diag[:, k, c, :], ident[:, :], conv_w_sb[:, k, c:c + 1], None, ALU.mult)
            for k in range(HH):
                dve.tensor_scalar(w2_diag[:, k, :], ident2[:, :], w2_sb[:, k:k + 1], None, ALU.mult)
            dve.memset(gT[M:M + 1, :], 1.0)
            dve.scalar_tensor_tensor(b1f[:, :], w1_sb[:, :], bin_sb[:, 0:1], b1_sb[:, :], ALU.mult, ALU.add)\
               .then_inc(const_dve, 1)

            def body(it, st):
                tile_x, tile_a, tile_b, half = it + 1, it, it - LAG_B, it - LAG_SCAN
                tile_p, tile_f, tile_o = it - LAG_POST, it - LAG_FFN, it - LAG_STORE
                for s in range(SLOTS):
                    i, d = s // KD, s % KD
                    if st["next_x"] and s == 5:
                        dve.wait_ge(x_in, 16 * tile_x + 16)
                        for q in range(SUB):
                            o = dve.bn_stats(x_stats[:, q, :], xt[:, q, :])
                        o.then_inc(x_stats_done, 1)
                    if st["ffn"] and s == 17:
                        dve.wait_ge(f_done, tile_f + 1)
                        for q in range(SUB):
                            o = dve.bn_stats(f_stats[:, q, :], ffn_bank[:, q * DM:(q + 1) * DM])
                        o.then_inc(f_stats_done, 1)
                    if st["post"] and s == 21:
                        dve.wait_ge(r_step, 2 * tile_p + 1)
                        for q in range(SUB):
                            o = dve.bn_stats(r_stats[:, q, :], r_sb[:, q, :])
                        o.then_inc(r_stats_done, 1)
                    if st["post"] and s == 27:
                        dve.wait_ge(x1_ready, tile_p + 1)
                        for q in range(SUB):
                            o = dve.bn_stats(x1_stats[:, q, :], x1[:, tile_p % 2, q, :])
                        o.then_inc(x1_stats_done, 1)
                    if st["scan"]:
                        slot = half * SLOTS + s
                        chunk = half // 2
                        hb = i % 2
                        if d == PAIR - 1:
                            wait(dve, hT_done, (half * HALF + i - 1) * 4)
                            if i == 0:
                                wait(dve, state_saved, half * HALF - HALF)
                        if s % PAIR == PAIR - 1:
                            dve.wait_ge(decay_ready, slot + 1)
                            dve.wait_ge(first_ready, (slot + 1) // PAIR)
                            dve.wait_ge(inp_ready, slot + 1)
                            pair = s // PAIR % (RING // PAIR)
                            dve.tensor_tensor_scan(h[:, hb, d - 1:d + 1, :].rearrange("p k t -> p (k t)")[:, 1:],
                                                   decay[:, pair, :, :].rearrange("p k t -> p (k t)")[:, 1:],
                                                   inp[:, pair, :, :].rearrange("p k t -> p (k t)")[:, 1:],
                                                   state[:, chunk % 2, (half * HALF + i) % NS, d - 1:d],
                                                   ALU.mult, ALU.add).then_inc(scan_done, PAIR)
                    if st["next_x"] and s == 5:
                        dve.wait_ge(x_stats_done, tile_x + 1)
                        dve.sem_inc(dve_waits_taken, 1)
                        for q in range(SUB):
                            o = dve.bn_aggr(x_mv[:, q, :], x_stats[:, q, :])
                        o.then_inc(x_mv_done, 1)
                    if st["ffn"] and s == 17:
                        dve.wait_ge(f_stats_done, tile_f + 1)
                        dve.sem_inc(dve_waits_taken, 1)
                        for q in range(SUB):
                            o = dve.bn_aggr(f_mv[:, q, :], f_stats[:, q, :])
                        o.then_inc(f_mv_done, 1)
                    if st["post"] and s == 21:
                        dve.wait_ge(r_stats_done, tile_p + 1)
                        dve.sem_inc(dve_waits_taken, 1)
                        for q in range(SUB):
                            o = dve.bn_aggr(r_mv[:, q, :], r_stats[:, q, :])
                        o.then_inc(r_mv_done, 1)
                    if st["post"] and s == 27:
                        dve.wait_ge(x1_stats_done, tile_p + 1)
                        dve.sem_inc(dve_waits_taken, 1)
                        for q in range(SUB):
                            o = dve.bn_aggr(x1_mv[:, q, :], x1_stats[:, q, :])
                        o.then_inc(x1_mv_done, 1)
                    if st["scan"] and (s > KD or st["before"]) or st["drain"] and s <= KD:
                        step = half * HALF + (s - 1) // KD - 1
                        da = (s - 1) % KD
                        idx = step * KD + da
                        dve.wait_ge(hT_done, idx + 1)
                        if KD < s <= 2 * KD:
                            dve.wait_ge(acc_init, (half // 2) * 4 + 4)
                        wait(dve, acc_done, idx - 3)
                        y = acc[:, bass.ds((step // NS % 2) * 4 + da, 1), :].rearrange("p o d -> p (o d)")
                        dve.scalar_tensor_tensor(y, hT_bank[da % 2][:, :], c_tok[:, step % (3 * NS), da:da + 1], y,
                                                 ALU.mult, ALU.add).then_inc(acc_done, 1)
                    if st["scan"] and d == KD - 1:
                        dve.wait_ge(scan_done, half * SLOTS + s + 1)
                        dve.tensor_scalar(state[:, 1, (half * HALF + i) % NS, :], h[:, hb, :, TC], 1.0, None, ALU.mult).then_inc(state_saved, 1)
                    if st["next_x"] and s == 5:
                        dve.wait_ge(x_mv_done, tile_x + 1)
                        slot8 = tile_x % 8
                        dve.tensor_scalar(x_norm[:, slot8, 0:2], x_mv[:, :, 0], -1.0, None, ALU.mult)
                        dve.tensor_scalar(x_norm[:, slot8, 2:4], x_mv[:, :, 1], EPS, None, ALU.add)
                        dve.tensor_scalar(x_norm[:, slot8, 4:6], x_mv[:, :, 1], 1.0 + EPS, EPS * EPS, ALU.mult, ALU.add)\
                           .then_inc(x_step, 1)
                    if st["next_x"] and s == 9:
                        dve.wait_ge(x_rstd, tile_x + 1)
                        wait(dve, xn_ready, tile_x)
                        dve.tensor_tensor(x_shift[:, :], x_norm[:, tile_x % 8, 0:2], x_norm[:, tile_x % 8, 4:6], ALU.mult)\
                           .then_inc(x_shifted, 1)
                    if st["prep_b"] and s in (11, 16):
                        q = (s == 16)
                        dve.wait_ge(e_ready, 2 * tile_b + 1 + q)
                        dve.tensor_scalar(e_sb[:, :, :], e_sb[:, :, :], EXP_CAP, None, ALU.min).then_inc(e_capped, 1)
                    if st["prep_b"] and s in (13, 18):
                        q = (s == 18)
                        dve.wait_ge(l_ready, 2 * tile_b + 1 + q)
                        if q == 0:
                            if st["scan"]:
                                wait(dve, decay_ready, (tile_b - 2) // 2 * (2 * SLOTS))
                        bnk = (lo_bank, hi_bank)[q]
                        for k in range(2):
                            o = dve.scalar_tensor_tensor(
                                dt_sb[:, tile_b // 2 % 2, 2 * q + k, bass.ds((tile_b % 2) * TT, TT)],
                                bnk[:, k * TT:(k + 1) * TT], b_dt_sb[:, 2 * q + k:2 * q + k + 1], e_sb[:, k, :],
                                ALU.add, ALU.max)
                        o.then_inc(dt_ready, 1)
                    if st["post"] and s == 20:
                        dve.wait_ge(xm_ready, tile_p + 1)
                        dve.wait_ge(proj_done, tile_p + 1)
                        wait(dve, rn_ready, tile_p)
                        for q in range(SUB):
                            o = dve.scalar_tensor_tensor(r_sb[:, q, :], xm[:, q, :], x_norm[:, tile_p % 8, 2 + q:3 + q],
                                                         post_bank[:, q * DM:(q + 1) * DM], ALU.mult, ALU.add)
                        o.then_inc(r_step, 1)
                    if st["post"] and s == 21:
                        dve.wait_ge(r_mv_done, tile_p + 1)
                        dve.tensor_scalar(r_std[:, 0, :], r_mv[:, :, 1], EPS, None, ALU.add).then_inc(r_step, 1)
                    if st["post"] and s == 23:
                        dve.wait_ge(r_rstd, tile_p + 1)
                        wait(dve, rn_ready, tile_p)
                        dve.scalar_tensor_tensor(r_shift[:, :], r_mv[:, :, 0], -1.0, r_std[:, 1, :], ALU.mult, ALU.mult)\
                           .then_inc(r_shifted, 1)
                    if st["post"] and s == 27:
                        dve.wait_ge(x1_mv_done, tile_p + 1)
                        dve.tensor_scalar(x1_std[:, 0, :], x1_mv[:, :, 1], EPS, None, ALU.add).then_inc(x1_step, 1)
                    if st["post"] and s == 29:
                        dve.wait_ge(x1_rstd, tile_p + 1)
                        wait(dve, x1T_done, tile_p)
                        for q in range(SUB):
                            o = dve.tensor_scalar(x1n[:, q, :], x1[:, tile_p % 2, q, :], x1_mv[:, q, 0:1],
                                                  x1_std[:, 1, q:q + 1], ALU.subtract, ALU.mult)
                        o.then_inc(x1n_ready, 1)
                    if st["ffn"] and s == 17:
                        dve.wait_ge(f_mv_done, tile_f + 1)
                        dve.tensor_scalar(f_std[:, 0, :], f_mv[:, :, 1], EPS, None, ALU.add).then_inc(f_step, 1)
                    if st["ffn"] and s == 19:
                        dve.wait_ge(f_rstd, tile_f + 1)
                        wait(dve, fo_ready, tile_f)
                        dve.scalar_tensor_tensor(f_shift[:, :], f_mv[:, :, 0], -1.0, f_std[:, 1, :], ALU.mult, ALU.mult)\
                           .then_inc(f_shifted, 1)

            over_iterations(dve, body)


N_WEIGHTS = 24

_INS = ["x", "w_in", "conv_w", "conv_b", "w_xproj", "w_dt", "b_dt", "A_log", "D", "w_out", "ln_g", "ln_b"]
_FFN = ["Win", "bin_", "W1", "b1", "W2", "b2", "Wout", "bout"]


def kernel(**inputs):
    import numpy as _np
    import concourse.bacc as _bacc
    from concourse import mybir as _mybir
    from concourse.bass_utils import run_bass_kernel_spmd as _run

    nc = _bacc.Bacc("TRN2", target_bir_lowering=False, num_devices=1)
    arrays, args = {}, []
    for name in ["L0_attn_" + n for n in _INS] + ["L0_ffn_" + n for n in _FFN]:
        a = _np.ascontiguousarray(inputs[name])
        arrays[f"in_{name}_dram"] = a
        args.append(nc.dram_tensor(f"in_{name}_dram", a.shape, _mybir.dt.from_np(a.dtype), kind="ExternalInput").ap())
    shape = inputs["L0_attn_x"].shape
    args.append(nc.dram_tensor("out_0_dram", shape, _mybir.dt.float32, kind="ExternalOutput").ap())
    bass_mamba_mlp_sandwich(nc, *args)
    r = _run(nc, [arrays], core_ids=[0])
    return r.results[0]["out_0_dram"]
```
